# Optimizing a Trainium2 kernel written in Bass

```python
import numpy as np
import jax
import jax.numpy as jnp

def _softmax(x, axis=-1):
    return jax.nn.softmax(x, axis=axis)

def _gelu(x):
    return jax.nn.gelu(x, approximate=True)

def _silu(x):
    return jax.nn.silu(x)

def _sigmoid(x):
    return jax.nn.sigmoid(x)

def _layernorm(x, axis=-1, eps=1e-05):
    m = jnp.mean(x, axis=axis, keepdims=True)
    v = jnp.var(x, axis=axis, keepdims=True)
    return (x - m) / jnp.sqrt(v + eps)

def _scatter_add(tgt, idx, src, axis=0):
    return tgt.at[idx].add(src)

def _segment_sum(src, seg, n):
    return jax.ops.segment_sum(src, seg, n)
kernel_name = 'mk_adaln_d1_jaxref_r8_b2aa2c'

def setup_inputs(seed: int=0):
    np.random.seed(seed)
    _w = jnp.asarray

    def _L0_attn_setup():
        import jax, jax.numpy as jnp
        import numpy as np
        D_MODEL = 128
        N_HEADS = 16
        D_HEAD = 64
        B, S = (8, 128)
        EPS = 1.1920929e-07
        key = jax.random.key(seed)
        k1, k2, k3 = jax.random.split(key, 3)
        x = jax.random.normal(k1, (B, S, D_MODEL), dtype=jnp.float32)
        W_qkv = jax.random.normal(k2, (3 * N_HEADS * D_HEAD, D_MODEL), dtype=jnp.float32) * 0.02
        b_qkv = jnp.zeros((3 * N_HEADS * D_HEAD,), dtype=jnp.float32)
        W_o = jax.random.normal(k3, (D_MODEL, N_HEADS * D_HEAD), dtype=jnp.float32) * 0.02
        b_o = jnp.zeros((D_MODEL,), dtype=jnp.float32)
        return {'x': x, 'W_qkv': W_qkv, 'b_qkv': b_qkv, 'W_o': W_o, 'b_o': b_o}
    _L0_attn_in = _L0_attn_setup()

    def _L0_ffn_setup():
        import jax, jax.numpy as jnp
        import numpy as np
        HIDDEN = 128
        N_EXPERTS = 32
        MOE_I = 64
        N_GROUP = 4
        TOPK_GROUP = 2
        TOP_K = 6
        N_LOCAL_GROUPS = 16
        ANCHOR_I = 32
        SHARED_I = 64
        ROUTED_SCALE = 0.2
        ANCHOR_ALPHA = 0.1
        BATCH, SEQ = (1, 128)

        def _moe_forward(hidden_states, gate_weight, gate_bias, w_gate, w_up, w_down, shared_w_gate, shared_w_up, shared_w_down, anchor_w_gate, anchor_w_up, anchor_w_down):
            B, S, H = hidden_states.shape
            x = hidden_states.reshape(-1, H)
            T = x.shape[0]
            E = gate_weight.shape[0]
            L = anchor_w_gate.shape[0]
            logits = x @ gate_weight.T
            scores = jax.nn.sigmoid(logits)
            sc = scores + gate_bias
            grp = sc.reshape(T, N_GROUP, E // N_GROUP)
            group_scores = jax.lax.top_k(grp, 2)[0].sum(-1)
            _, gidx = jax.lax.top_k(group_scores, TOPK_GROUP)
            gmask = jax.nn.one_hot(gidx, N_GROUP, dtype=sc.dtype).sum(1)
            emask = jnp.repeat(gmask, E // N_GROUP, axis=1)
            masked = jnp.where(emask > 0, sc, -jnp.inf)
            _, topidx = jax.lax.top_k(masked, TOP_K)
            tw = jnp.take_along_axis(scores, topidx, axis=-1)
            tw = tw / (tw.sum(-1, keepdims=True) + 1e-20) * ROUTED_SCALE
            g = jnp.einsum('th,ehi->tei', x, w_gate)
            u = jnp.einsum('th,ehi->tei', x, w_up)
            eo = jnp.einsum('tei,eih->teh', jax.nn.silu(g) * u, w_down)
            cw = (jax.nn.one_hot(topidx, E, dtype=x.dtype) * tw[..., None]).sum(1)
            routed = jnp.einsum('te,teh->th', cw, eo)
            shared = jax.nn.silu(x @ shared_w_gate) * (x @ shared_w_up) @ shared_w_down
            lg = topidx[:, 0] // (E // L)
            ag = jnp.einsum('th,lhi->tli', x, anchor_w_gate)
            au = jnp.einsum('th,lhi->tli', x, anchor_w_up)
            ao = jnp.einsum('tli,lih->tlh', jax.nn.silu(ag) * au, anchor_w_down)
            acw = jax.nn.one_hot(lg, L, dtype=x.dtype)
            anchor = jnp.einsum('tl,tlh->th', acw, ao)
            out = routed + shared + ANCHOR_ALPHA * anchor
            return out.reshape(B, S, H)
        key = jax.random.key(seed)
        ks = jax.random.split(key, 13)
        s = 0.02
        return {'hidden_states': jax.random.normal(ks[0], (BATCH, SEQ, HIDDEN), jnp.float32), 'gate_weight': s * jax.random.normal(ks[1], (N_EXPERTS, HIDDEN), jnp.float32), 'gate_bias': s * jax.random.normal(ks[2], (N_EXPERTS,), jnp.float32), 'w_gate': s * jax.random.normal(ks[3], (N_EXPERTS, HIDDEN, MOE_I), jnp.float32), 'w_up': s * jax.random.normal(ks[4], (N_EXPERTS, HIDDEN, MOE_I), jnp.float32), 'w_down': s * jax.random.normal(ks[5], (N_EXPERTS, MOE_I, HIDDEN), jnp.float32), 'shared_w_gate': s * jax.random.normal(ks[6], (HIDDEN, SHARED_I), jnp.float32), 'shared_w_up': s * jax.random.normal(ks[7], (HIDDEN, SHARED_I), jnp.float32), 'shared_w_down': s * jax.random.normal(ks[8], (SHARED_I, HIDDEN), jnp.float32), 'anchor_w_gate': s * jax.random.normal(ks[9], (N_LOCAL_GROUPS, HIDDEN, ANCHOR_I), jnp.float32), 'anchor_w_up': s * jax.random.normal(ks[10], (N_LOCAL_GROUPS, HIDDEN, ANCHOR_I), jnp.float32), 'anchor_w_down': s * jax.random.normal(ks[11], (N_LOCAL_GROUPS, ANCHOR_I, HIDDEN), jnp.float32)}
    _L0_ffn_in = _L0_ffn_setup()
    _L0_c = _w((lambda *s: np.random.randn(*s).astype(np.float32) * 0.05)(32, 128))
    _L0_wmod = _w((lambda *s: np.random.randn(*s).astype(np.float32) * 0.05)(128, 6 * 128) * 128 ** (-0.5))
    _d = {'L0_attn_x': _L0_attn_in['x'], 'L0_attn_W_qkv': _L0_attn_in['W_qkv'], 'L0_attn_b_qkv': _L0_attn_in['b_qkv'], 'L0_attn_W_o': _L0_attn_in['W_o'], 'L0_attn_b_o': _L0_attn_in['b_o'], 'L0_ffn_gate_weight': _L0_ffn_in['gate_weight'], 'L0_ffn_gate_bias': _L0_ffn_in['gate_bias'], 'L0_ffn_w_gate': _L0_ffn_in['w_gate'], 'L0_ffn_w_up': _L0_ffn_in['w_up'], 'L0_ffn_w_down': _L0_ffn_in['w_down'], 'L0_ffn_shared_w_gate': _L0_ffn_in['shared_w_gate'], 'L0_ffn_shared_w_up': _L0_ffn_in['shared_w_up'], 'L0_ffn_shared_w_down': _L0_ffn_in['shared_w_down'], 'L0_ffn_anchor_w_gate': _L0_ffn_in['anchor_w_gate'], 'L0_ffn_anchor_w_up': _L0_ffn_in['anchor_w_up'], 'L0_ffn_anchor_w_down': _L0_ffn_in['anchor_w_down'], 'L0_c': _L0_c, 'L0_wmod': _L0_wmod}
    _x0 = _d['L0_attn_x']
    _d['L0_attn_x'] = jax.random.normal(jax.random.fold_in(jax.random.key(seed), 1), (32, 256, 128), dtype=_x0.dtype)
    del _x0
    return _d

def reference(L0_attn_x, L0_attn_W_qkv, L0_attn_b_qkv, L0_attn_W_o, L0_attn_b_o, L0_ffn_gate_weight, L0_ffn_gate_bias, L0_ffn_w_gate, L0_ffn_w_up, L0_ffn_w_down, L0_ffn_shared_w_gate, L0_ffn_shared_w_up, L0_ffn_shared_w_down, L0_ffn_anchor_w_gate, L0_ffn_anchor_w_up, L0_ffn_anchor_w_down, L0_c, L0_wmod):

    def _L0_attn_ref(x, W_qkv, b_qkv, W_o, b_o):
        import jax, jax.numpy as jnp
        import numpy as np
        D_MODEL = 128
        N_HEADS = 16
        D_HEAD = 64
        B, S = (8, 128)
        EPS = 1.1920929e-07
        normed = x * jax.lax.rsqrt(jnp.mean(x * x, axis=-1, keepdims=True) + EPS)
        qkv = normed @ W_qkv.T + b_qkv
        qkv = qkv.reshape(*qkv.shape[:-1], N_HEADS, D_HEAD, 3)
        q, k, v = (qkv[..., 0], qkv[..., 1], qkv[..., 2])
        scores = jnp.einsum('bqhd,bkhd->bhqk', q, k)
        seq = x.shape[-2]
        causal_mask = jnp.triu(jnp.ones((seq, seq), dtype=bool), k=1)
        scores = jnp.where(causal_mask, -jnp.inf, scores)
        attn = jax.nn.softmax(scores, axis=-2)
        z = jnp.einsum('bhqk,bkhd->bqhd', attn, v)
        z = z.reshape(*z.shape[:-2], N_HEADS * D_HEAD)
        return z @ W_o.T + b_o

    def _L0_ffn_ref(hidden_states, gate_weight, gate_bias, w_gate, w_up, w_down, shared_w_gate, shared_w_up, shared_w_down, anchor_w_gate, anchor_w_up, anchor_w_down):
        import jax, jax.numpy as jnp
        import numpy as np
        HIDDEN = 128
        N_EXPERTS = 32
        MOE_I = 64
        N_GROUP = 4
        TOPK_GROUP = 2
        TOP_K = 6
        N_LOCAL_GROUPS = 16
        ANCHOR_I = 32
        SHARED_I = 64
        ROUTED_SCALE = 0.2
        ANCHOR_ALPHA = 0.1
        BATCH, SEQ = (1, 128)

        def _moe_forward(hidden_states, gate_weight, gate_bias, w_gate, w_up, w_down, shared_w_gate, shared_w_up, shared_w_down, anchor_w_gate, anchor_w_up, anchor_w_down):
            B, S, H = hidden_states.shape
            x = hidden_states.reshape(-1, H)
            T = x.shape[0]
            E = gate_weight.shape[0]
            L = anchor_w_gate.shape[0]
            logits = x @ gate_weight.T
            scores = jax.nn.sigmoid(logits)
            sc = scores + gate_bias
            grp = sc.reshape(T, N_GROUP, E // N_GROUP)
            group_scores = jax.lax.top_k(grp, 2)[0].sum(-1)
            _, gidx = jax.lax.top_k(group_scores, TOPK_GROUP)
            gmask = jax.nn.one_hot(gidx, N_GROUP, dtype=sc.dtype).sum(1)
            emask = jnp.repeat(gmask, E // N_GROUP, axis=1)
            masked = jnp.where(emask > 0, sc, -jnp.inf)
            _, topidx = jax.lax.top_k(masked, TOP_K)
            tw = jnp.take_along_axis(scores, topidx, axis=-1)
            tw = tw / (tw.sum(-1, keepdims=True) + 1e-20) * ROUTED_SCALE
            g = jnp.einsum('th,ehi->tei', x, w_gate)
            u = jnp.einsum('th,ehi->tei', x, w_up)
            eo = jnp.einsum('tei,eih->teh', jax.nn.silu(g) * u, w_down)
            cw = (jax.nn.one_hot(topidx, E, dtype=x.dtype) * tw[..., None]).sum(1)
            routed = jnp.einsum('te,teh->th', cw, eo)
            shared = jax.nn.silu(x @ shared_w_gate) * (x @ shared_w_up) @ shared_w_down
            lg = topidx[:, 0] // (E // L)
            ag = jnp.einsum('th,lhi->tli', x, anchor_w_gate)
            au = jnp.einsum('th,lhi->tli', x, anchor_w_up)
            ao = jnp.einsum('tli,lih->tlh', jax.nn.silu(ag) * au, anchor_w_down)
            acw = jax.nn.one_hot(lg, L, dtype=x.dtype)
            anchor = jnp.einsum('tl,tlh->th', acw, ao)
            out = routed + shared + ANCHOR_ALPHA * anchor
            return out.reshape(B, S, H)
        return _moe_forward(hidden_states, gate_weight, gate_bias, w_gate, w_up, w_down, shared_w_gate, shared_w_up, shared_w_down, anchor_w_gate, anchor_w_up, anchor_w_down)
    x = L0_attn_x
    mod = (_silu(L0_c) @ L0_wmod).reshape(L0_c.shape[0], 6, 1, -1)
    sa, ca, ga, sb, cb, gb = (mod[:, 0], mod[:, 1], mod[:, 2], mod[:, 3], mod[:, 4], mod[:, 5])
    ga = (2 * (ga >= 0) - 1) * jnp.maximum(jnp.abs(ga), 0.25)
    gb = (2 * (gb >= 0) - 1) * jnp.maximum(jnp.abs(gb), 0.25)
    h = _layernorm(x, axis=-1) * (1 + ca) + sa
    x = x + ga * _L0_attn_ref(h, L0_attn_W_qkv, L0_attn_b_qkv, L0_attn_W_o, L0_attn_b_o)
    h = _layernorm(x, axis=-1) * (1 + cb) + sb
    x = x + gb * _L0_ffn_ref(h, L0_ffn_gate_weight, L0_ffn_gate_bias, L0_ffn_w_gate, L0_ffn_w_up, L0_ffn_w_down, L0_ffn_shared_w_gate, L0_ffn_shared_w_up, L0_ffn_shared_w_down, L0_ffn_anchor_w_gate, L0_ffn_anchor_w_up, L0_ffn_anchor_w_down)
    return x

_drawn_inputs = setup_inputs


def setup_inputs(seed=0):
    import zlib

    import numpy as np

    out = dict(_drawn_inputs(seed))
    spreads = {'L0_attn_b_qkv': (0.0, 0.397), 'L0_attn_b_o': (0.0, 0.306)}
    factors = {'L0_attn_W_qkv': 7.509,
     'L0_ffn_gate_weight': 8.0,
     'L0_ffn_gate_bias': 8.0,
     'L0_ffn_w_gate': 8.0,
     'L0_ffn_w_up': 8.0,
     'L0_ffn_w_down': 8.0,
     'L0_ffn_shared_w_gate': 8.0,
     'L0_ffn_shared_w_up': 8.0,
     'L0_ffn_shared_w_down': 8.0,
     'L0_ffn_anchor_w_gate': 8.0,
     'L0_ffn_anchor_w_up': 8.0,
     'L0_ffn_anchor_w_down': 8.0}
    for name, (base, spread) in spreads.items():
        noise = np.random.default_rng([zlib.crc32(name.encode()), seed]).standard_normal(out[name].shape)
        drawn = base * np.exp(spread * noise) if base else spread * noise
        out[name] = jnp.asarray(drawn.astype(out[name].dtype))
    for name, factor in factors.items():
        out[name] = (out[name] * factor).astype(out[name].dtype)
    return out
```

```python
from contextlib import ExitStack

import concourse.bass as bass
from concourse import mybir

ALU = mybir.AluOpType
ACT = mybir.ActivationFunctionType
F32 = mybir.dt.float32
F32R = mybir.dt.float32r
U32 = mybir.dt.uint32
AX_X = mybir.AxisListType.X

P = 128
LN_EPS = 1e-05
RMS_EPS = 1.1920929e-07
ROUTED_SCALE = 0.2
ANCHOR_ALPHA = 0.1
TOP_K = 6
N_GROUP = 4
BIG = 1e30


def adaln_block_kernel(nc, x, W_qkv, b_qkv, W_o, b_o, gate_w, gate_bias, w_gate, w_up, w_down,
                       sh_gate, sh_up, sh_down, an_gate, an_up, an_down, cond, wmod, out):
    NB, S, D = x.shape
    KT = S // P
    HD = W_o.shape[1]
    DH = 64
    PAIRS = HD // P
    E, _, EI = w_gate.shape
    L, _, AI = an_gate.shape
    ET = E * EI // P
    AT = L * AI // P
    WT = ET + AT
    FT = WT + 1
    SW = S + P
    CH = 512
    NCH = NB * S // CH
    TPC = CH // P
    SPC = CH // S
    RW = E + L
    NORM_STEPS = 12

    mod_dram = nc.dram_tensor("mod_rows", (NB, 2 * D), F32, kind="Internal").ap()

    with ExitStack() as ctx:
        memory = ctx

        def sb(name, shape, dt=F32):
            return memory.enter_context(nc.sbuf_tensor(name, shape, dt))

        def pb(name):
            return ctx.enter_context(nc.psum_tensor(name, [P, 512], F32))

        def sem(name):
            return ctx.enter_context(nc.semaphore(name))

        ident = sb("ident", [P, P])
        ones = sb("ones", [P, P])
        causal = sb("causal", [P, SW])
        earlier = sb("earlier", [P, N_GROUP, N_GROUP])
        iota_e = sb("iota_e", [P, E])
        unused = sb("unused", [P, 8])
        half_pow = sb("half_pow", [P, TPC])
        pick = sb("pick", [P, WT, P], F32R)
        wqk_hi = sb("wqk_hi", [P, 2, PAIRS, P], F32R)
        wqk_lo = sb("wqk_lo", [P, 2, PAIRS, P], F32R)
        wv_hi = sb("wv_hi", [P, HD], F32R)
        wv_lo = sb("wv_lo", [P, HD], F32R)
        woT = sb("woT", [P, PAIRS, D])
        bqkv = sb("bqkv", [P, PAIRS, 3])
        nbq = sb("nbq", [P, PAIRS])
        bv_diag = sb("bv_diag", [P, 2, P])
        bv_rows = sb("bv_rows", [P, HD])
        bo_col = sb("bo_col", [P, 1])
        bias_row = sb("bias_row", [P, E])
        wgu_hi = sb("wgu_hi", [P, 2, FT, P], F32R)
        wgu_lo = sb("wgu_lo", [P, 2, FT, P], F32R)
        wd_hi = sb("wd_hi", [P, FT, D], F32R)
        wd_lo = sb("wd_lo", [P, FT, D], F32R)
        gwT_hi = sb("gwT_hi", [P, E], F32R)
        gwT_lo = sb("gwT_lo", [P, E], F32R)
        modT = sb("modT", [P, 6, NB])
        mod_tmp = sb("mod_tmp", [P, 2, NB])
        gaT = sb("gaT", [P, NB])
        gbT = sb("gbT", [P, NB])
        x_all = sb("x_all", [P, NB * KT, D])

        memory = ExitStack()
        bnst = sb("bnst", [P, TPC, 6])
        mv = sb("mv", [P, TPC, 2])
        var_eps = sb("var_eps", [P, TPC])
        rstd = sb("rstd", [P, TPC])
        sumsq = sb("sumsq", [P, KT])
        ms_eps = sb("ms_eps", [P, KT])
        rrms = sb("rrms", [P, KT])
        sq_junk = sb("sq_junk", [P, KT, D])
        xhat = sb("xhat", [P, TPC, D])
        hmod = sb("hmod", [P, KT, D])
        hmul = sb("hmul", [P, KT, D])
        normed = sb("normed", [P, KT, D])
        mod_bc = sb("mod_bc", [P, 2, 2 * D])
        nT_hi = sb("nT_hi", [P, 2, S], F32R)
        nT_lo = sb("nT_lo", [P, 2, S], F32R)
        qk_hi = sb("qk_hi", [P, 2, 2, S], F32R)
        qk_lo = sb("qk_lo", [P, 2, 2, S], F32R)
        v_sb = sb("v_sb", [P, 2, KT, HD])
        vn = sb("vn", [P, 2, KT, P])
        s_sb = sb("s_sb", [P, 4, SW])
        smin = sb("smin", [P, 4, KT])
        zsum = sb("zsum", [P, 2, KT, 2])
        rz = sb("rz", [P, 2, KT, 2])
        zT = sb("zT", [P, 2, PAIRS, S])
        attT = sb("attT", [P, S])

        memory.close()
        memory = ctx

        mv2 = sb("mv2", [P, TPC, 2])
        bnst2 = sb("bnst2", [P, TPC, 6])
        var_eps2 = sb("var_eps2", [P, TPC])
        rstd2 = sb("rstd2", [P, TPC])
        xhat2 = sb("xhat2", [P, TPC, D])
        hT = sb("hT", [P, CH])
        hT_hi = sb("hT_hi", [P, 2, CH], F32R)
        hT_lo = sb("hT_lo", [P, 2, CH], F32R)
        sig = sb("sig", [P, TPC, E])
        sel = sb("sel", [P, TPC, E])
        dup = sb("dup", [P, TPC * N_GROUP, E // N_GROUP])
        masked = sb("masked", [P, TPC, E])
        gtop = sb("gtop", [P, 6, TPC, N_GROUP])
        ge4 = sb("ge4", [P, TPC, N_GROUP, N_GROUP])
        gt4 = sb("gt4", [P, TPC, N_GROUP, N_GROUP])
        top8 = sb("top8", [P, TPC, 8])
        idx8 = sb("idx8", [P, TPC, 8], U32)
        idxf = sb("idxf", [P, TPC, TOP_K])
        chosen = sb("chosen", [P, TPC, TOP_K, E])
        cw = sb("cw", [P, TPC, RW])
        wsum = sb("wsum", [P, 2, TPC])
        cw_parts = sb("cw_parts", [P, TPC, 2 * RW], F32R)
        cwT = sb("cwT", [2 * RW, 2, CH], F32R)
        act_sb = sb("act_sb", [P, 2, CH])
        prod_sb = sb("prod_sb", [P, 2, CH])
        hid = sb("hid", [P, 3, CH])
        hid_hi = sb("hid_hi", [P, 3, CH], F32R)
        hid_lo = sb("hid_lo", [P, 3, CH], F32R)
        yT = sb("yT", [P, CH])

        banks = [pb(f"bank{i}") for i in range(8)]
        pQK, pS, pZ, pM = banks[0:2], banks[2:6], banks[6], banks[7]

        x_first = sem("x_first")
        x_loaded = sem("x_loaded")
        w_loaded = sem("w_loaded")
        mod_loaded = sem("mod_loaded")
        bias_loaded = sem("bias_loaded")
        consts_made = sem("consts_made")
        pick_made = sem("pick_made")
        silu_c_done = sem("silu_c_done")
        pro_pe = sem("pro_pe")
        pro_ev = sem("pro_ev")
        pro_step = sem("pro_step")
        mod_rows_made = sem("mod_rows_made")
        nbq_made = sem("nbq_made")
        bv_diag_made = sem("bv_diag_made")
        mod_stored = sem("mod_stored")
        raw_loaded = sem("raw_loaded")
        raw_hi = sem("raw_hi")
        raw_lo = sem("raw_lo")
        mod_rows_in = [sem(f"mod_rows_in{i}") for i in range(2)]
        norm_step = sem("norm_step")
        pow_done = sem("pow_done")
        hmod_step = sem("hmod_step")
        nT_ps = sem("nT_ps")
        nT_hi_done = sem("nT_hi_done")
        nT_lo_done = sem("nT_lo_done")
        qk_ps = sem("qk_ps")
        qk_hi_done = sem("qk_hi_done")
        qk_lo_done = sem("qk_lo_done")
        s_ps = sem("s_ps")
        s_masked = sem("s_masked")
        e_done = sem("e_done")
        rz_done = sem("rz_done")
        vn_done = sem("vn_done")
        v_ps = sem("v_ps")
        v_done = sem("v_done")
        z_ps = sem("z_ps")
        z_done = sem("z_done")
        o_ps = sem("o_ps")
        att_done = sem("att_done")
        attT_ps = sem("attT_ps")
        x_added = sem("x_added")
        ln_step = sem("ln_step")
        pow2_done = sem("pow2_done")
        xT_ps = sem("xT_ps")
        hT_done = sem("hT_done")
        hT_hi_done = sem("hT_hi_done")
        hT_lo_done = sem("hT_lo_done")
        logit_ps = sem("logit_ps")
        sig_done = sem("sig_done")
        route_step = sem("route_step")
        cwT_ps = sem("cwT_ps")
        cwT_done = sem("cwT_done")
        g_ps = sem("g_ps")
        u_ps = sem("u_ps")
        c_ps = sem("c_ps")
        silu_done = sem("silu_done")
        au_done = sem("au_done")
        hid_done = sem("hid_done")
        hid_hi_done = sem("hid_hi_done")
        hid_lo_done = sem("hid_lo_done")
        down_done = sem("down_done")
        yT_done = sem("yT_done")
        yT_ps = sem("yT_ps")
        y_done = sem("y_done")
        y_stored = sem("y_stored")

        wq_rows = v_sb[:].rearrange("p a k n -> p (a k n)")[:, 0:PAIRS * 3 * P].rearrange(
            "p (j c i) -> p j c i", j=PAIRS, c=3)
        wo_rows = v_sb[:].rearrange("p a k n -> p (a k n)")[:, PAIRS * 3 * P:PAIRS * 4 * P]
        wmod_sb = zT[:].rearrange("p a j s -> p (a j s)")[:, 0:6 * D]
        c_sb = zT[:].rearrange("p a j s -> p (a j s)")[0:NB, 6 * D:7 * D]
        sc_sb = zT[:].rearrange("p a j s -> p (a j s)")[0:NB, 7 * D:8 * D]
        gw_rows = zT[:].rearrange("p a j s -> p (a j s)")[0:E, 8 * D:9 * D]
        scT = zT[:].rearrange("p a j s -> p (a j s)")[:, 9 * D:9 * D + NB]
        mod_rows = zT[:].rearrange("p a j s -> p (a j s)")[0:NB, 10 * D:12 * D]
        stage = zT[:].rearrange("p a j s -> p (a j s)")[:, 0:FT * P]
        stage_gu = stage.rearrange("p (t n) -> p t n", n=P)

        def raw_lot(n):
            if n < 2:
                w, a, s = ((w_gate, an_gate, sh_gate), (w_up, an_up, sh_up))[n]
                return [
                    (stage[:, 0:ET * P].rearrange("p (e i) -> p e i", i=EI), w.rearrange("e h i -> h e i")),
                    (stage[:, ET * P:WT * P].rearrange("p (l i) -> p l i", i=AI), a.rearrange("l h i -> h l i")),
                    (stage[:, WT * P:WT * P + EI], s),
                ]
            return [
                (stage_gu[:, 0:ET, :], w_down.rearrange("(t e) i h -> (e i) t h", e=P // EI)),
                (stage_gu[:, ET:WT, :], an_down.rearrange("(t l) i h -> (l i) t h", l=P // AI)),
                (stage_gu[0:EI, WT, :], sh_down),
            ]

        RAW_LOTS = 3
        raw_dst = [(wgu_hi[:, 0], wgu_lo[:, 0]), (wgu_hi[:, 1], wgu_lo[:, 1]), (wd_hi[:], wd_lo[:])]

        block = ctx.enter_context(nc.Block())
        last_b = NB - 1

        def each_sequence(eng, body):
            body(0, 0)
            body(1, 1)
            with eng.Fori(1, NB // 2 - 1) as i:
                body(i * 2, 0)
                body(i * 2 + 1, 1)
            body(NB - 2, 0)
            body(NB - 1, 1)

        def is_first(b):
            return isinstance(b, int) and b == 0

        def is_last(b):
            return isinstance(b, int) and b == last_b

        def each_chunk(eng, body):
            body(0, 0)
            body(1, 1)
            with eng.Fori(1, NCH // 2 - 1) as i:
                body(i * 2, 0)
                body(i * 2 + 1, 1)
            body(NCH - 2, 0)
            body(NCH - 1, 1)

        def wait_apart(eng, semaphore, count, cell):
            eng.wait_ge(semaphore, count)
            if not isinstance(count, int):
                eng.memset(unused[:, cell:cell + 1], 0.0)

        def below(n, limit):
            return isinstance(n, int) and n < limit


        pG, pU, pC, pY = banks[0:2], banks[2:4], banks[4:6], banks[6]
        LN_STEPS = 13
        ROUTE_STEPS = 32

        def ffn_pool(pool):
            pool.wait_ge(x_added, NB)

            def rstd_of(c):
                pool.wait_ge(ln_step, c * LN_STEPS + 9)
                pool.tensor_tensor(rstd2[:], var_eps2[:], half_pow[:], ALU.pow).then_inc(pow2_done, 1)

            def input_low(c, par):
                pool.wait_ge(hT_hi_done, c + 1)
                pool.tensor_tensor(hT_lo[:, par], hT[:], hT_hi[:, par].bitcast(F32), ALU.subtract).then_inc(hT_lo_done, 1)

            def hidden_low(T, t):
                pool.wait_ge(hid_hi_done, T + 1)
                if not below(T, 3):
                    pool.wait_ge(down_done, T - 2)
                pool.tensor_tensor(hid_lo[:, t % 3], hid[:, t % 3], hid_hi[:, t % 3].bitcast(F32),
                                   ALU.subtract).then_inc(hid_lo_done, 1)

            rstd_of(0)
            input_low(0, 0)

            def chunk(c, par):
                for t in range(FT):
                    hidden_low(c * FT + t, t)
                    if not (isinstance(c, int) and c == NCH - 1):
                        if t == 2:
                            rstd_of(c + 1)
                        if t == 6:
                            input_low(c + 1, 1 - par)

            each_chunk(pool, chunk)

        def ffn_tensor(pe):
            pe.wait_ge(x_added, NB)

            def input_transposes(c):
                pe.wait_ge(ln_step, c * LN_STEPS + LN_STEPS)
                for k in range(TPC):
                    ins = pe.transpose(pM[:, k * P:(k + 1) * P], xhat2[:, k, :], ident[:])
                ins.then_inc(xT_ps, 1)

            def logits(c, par):
                pe.wait_ge(hT_lo_done, c + 1)
                for k in range(TPC):
                    toks = slice(k * P, (k + 1) * P)
                    ins = three(pe, pM[:, k * E:(k + 1) * E], hT_hi[:, par, toks], hT_lo[:, par, toks], gwT_hi[:], gwT_lo[:])
                ins.then_inc(logit_ps, 1)

            def weight_transposes(c):
                pe.wait_ge(route_step, c * ROUTE_STEPS + ROUTE_STEPS)
                for k in range(TPC):
                    ins = pe.transpose(pM[0:2 * RW, k * P:(k + 1) * P], cw_parts[:, k, :].bitcast(F32), ident[:])
                ins.then_inc(cwT_ps, 1)

            def gate_up(T, t, par, q):
                for w, (dst, free, done) in enumerate(((pG[q], silu_done, g_ps), (pU[q], au_done, u_ps))):
                    if not below(T, 2):
                        pe.wait_ge(free, T - 1)
                    three(pe, dst[:], wgu_hi[:, w, t, :], wgu_lo[:, w, t, :], hT_hi[:, par], hT_lo[:, par]).then_inc(done, 1)

            def weights_out(T, t, par):
                if t >= 2:
                    pe.wait_ge(hid_done, T - 1)
                elif not below(T, FT):
                    pe.wait_ge(hid_done, T - 2)
                pe.matmul(pC[t % 2][:], pick[0:2 * RW, t, :], cwT[:, par, :], start=True, stop=True).then_inc(c_ps, 1)

            def down(T, t, c):
                pe.wait_ge(hid_lo_done, T + 1)
                if t == 0 and not (isinstance(c, int) and c == 0):
                    pe.wait_ge(yT_done, c)
                K = P if t < WT else EI
                three(pe, pY[:], wd_hi[0:K, t, :], wd_lo[0:K, t, :], hid_hi[0:K, t % 3], hid_lo[0:K, t % 3],
                      start=(t == 0), stop=(t == FT - 1)).then_inc(down_done, 1)

            def result_transposes(c):
                pe.wait_ge(yT_done, c + 1)
                if not (isinstance(c, int) and c == NCH - 1):
                    pe.wait_ge(cwT_done, c + 2)
                for k in range(TPC):
                    ins = pe.transpose(pM[:, k * P:(k + 1) * P], yT[:, k * P:(k + 1) * P], ident[:])
                ins.then_inc(yT_ps, 1)

            input_transposes(0)
            logits(0, 0)
            weight_transposes(0)

            def chunk(c, par):
                first, last = isinstance(c, int) and c == 0, isinstance(c, int) and c == NCH - 1
                for t in range(FT):
                    T = c * FT + t
                    if t == 0:
                        pe.wait_ge(cwT_done, c + 1)
                    gate_up(T, t, par, (FT * par + t) % 2)
                    if t < WT:
                        weights_out(T, t, par)
                    if t >= 2:
                        down(T - 2, t - 2, c)
                    elif not first:
                        down(T - 2, t - 2 + FT, c - 1)
                    if t == 3 and not first:
                        result_transposes(c - 1)
                    if not last:
                        if t == 5:
                            if not first:
                                pe.wait_ge(y_done, c)
                            input_transposes(c + 1)
                        if t == 9:
                            logits(c + 1, 1 - par)
                        if t == 17:
                            weight_transposes(c + 1)

            each_chunk(pe, chunk)
            for t in (FT - 2, FT - 1):
                down((NCH - 1) * FT + t, t, NCH - 1)
            pe.wait_ge(y_done, NCH - 1)
            result_transposes(NCH - 1)

        def ffn_scalar(act):
            act.wait_ge(x_added, NB)

            def input_high(c, par):
                act.wait_ge(hT_done, c * 2 + 2)
                act.activation(hT_hi[:, par], hT[:], ACT.Copy).then_inc(hT_hi_done, 1)

            def scores_out(c):
                act.wait_ge(logit_ps, c + 1)
                act.activation(sig[:], pM[:, 0:TPC * E].rearrange("p (k e) -> p k e", k=TPC), ACT.Sigmoid).then_inc(sig_done, 1)

            def weights_in(c, par):
                act.wait_ge(cwT_ps, c + 1)
                act.activation(cwT[:, par, :], pM[0:2 * RW, :], ACT.Copy).then_inc(cwT_done, 1)

            def gate_silu(T, q):
                act.wait_ge(g_ps, T + 1)
                if not below(T, 2):
                    act.wait_ge(au_done, T - 1)
                act.activation(act_sb[:, q], pG[q][:], ACT.Silu).then_inc(silu_done, 1)

            def hidden_high(T, t):
                act.wait_ge(hid_done, T + 1)
                if not below(T, 3):
                    act.wait_ge(down_done, T - 2)
                act.activation(hid_hi[:, t % 3], hid[:, t % 3], ACT.Copy).then_inc(hid_hi_done, 1)

            input_high(0, 0)
            scores_out(0)
            weights_in(0, 0)

            def chunk(c, par):
                first, last = isinstance(c, int) and c == 0, isinstance(c, int) and c == NCH - 1
                for t in range(FT):
                    T = c * FT + t
                    if t:
                        hidden_high(T - 1, t - 1)
                    elif not first:
                        hidden_high(T - 1, FT - 1)
                    gate_silu(T, (FT * par + t) % 2)
                    if not last:
                        if t == 6:
                            input_high(c + 1, 1 - par)
                        if t == 10:
                            scores_out(c + 1)
                        if t == 18:
                            weights_in(c + 1, 1 - par)

            each_chunk(act, chunk)
            hidden_high(NCH * FT - 1, FT - 1)

        def ffn_vector(dve):
            def layer_norm(c, part):
                def xt(k):
                    return x_all[:, bass.ds(c * TPC + k, 1), :].rearrange("p a d -> p (a d)")

                base = c * LN_STEPS
                if part == 0:
                    for k in range(TPC):
                        dve.bn_stats(bnst2[:, k, :], xt(k)).then_inc(ln_step, 1)
                    wait_apart(dve, ln_step, base + 4, 5)
                    for k in range(TPC):
                        dve.bn_aggr(mv2[:, k, :], bnst2[:, k, :]).then_inc(ln_step, 1)
                    dve.wait_ge(ln_step, base + 8)
                    dve.tensor_scalar(var_eps2[:], mv2[:, :, 1], LN_EPS, None, ALU.add).then_inc(ln_step, 1)
                else:
                    dve.wait_ge(pow2_done, c + 1)
                    for k in range(TPC):
                        dve.tensor_scalar(xhat2[:, k, :], xt(k), mv2[:, k, 0:1], rstd2[:, k:k + 1],
                                          ALU.subtract, ALU.mult).then_inc(ln_step, 1)

            def input_out(c):
                dve.wait_ge(xT_ps, c + 1)
                for s in range(SPC):
                    toks = slice(s * S, (s + 1) * S)
                    dve.tensor_scalar(hT[:, toks], pM[:, toks], modT[:, 4, bass.ds(c * SPC + s, 1)],
                                      modT[:, 3, bass.ds(c * SPC + s, 1)], ALU.mult, ALU.add).then_inc(hT_done, 1)

            def route(c, parts):
                base, n = c * ROUTE_STEPS, [ROUTE_AT[parts]]

                def then(ins, wait=True):
                    n[0] += 1
                    ins.then_inc(route_step, 1)
                    if wait:
                        dve.wait_ge(route_step, base + n[0])

                G8 = E // N_GROUP
                grouped = sel[:].rearrange("p k (g e) -> p (k g) e", e=G8)
                m1, m2, cnt, t1, t2, rank = [gtop[:, i].rearrange("p k g -> p (k g)") for i in range(6)]

                def over_e(v):
                    return v.rearrange("p (a b) -> p a b", b=1).broadcast_to([P, TPC * N_GROUP, G8])

                if parts == 0:
                    dve.wait_ge(sig_done, c + 1)
                    then(dve.tensor_tensor(sel[:], sig[:], bias_row[:].rearrange("p (a e) -> p a e", a=1).broadcast_to([P, TPC, E]), ALU.add))
                    then(dve.tensor_reduce(m1, grouped, AX_X, ALU.max))
                    then(dve.tensor_tensor(dup[:], grouped, over_e(m1), ALU.is_equal))
                    then(dve.tensor_reduce(cnt, dup[:], AX_X, ALU.add))
                    then(dve.scalar_tensor_tensor(out=dup[:], in0=dup[:], scalar=-BIG, in1=grouped, op0=ALU.mult, op1=ALU.add))
                    then(dve.tensor_reduce(m2, dup[:], AX_X, ALU.max))
                    then(dve.tensor_scalar(t1, cnt, 1.5, BIG, ALU.is_ge, ALU.mult))
                    then(dve.scalar_tensor_tensor(out=t2, in0=t1, scalar=-BIG, in1=m1, op0=ALU.add, op1=ALU.add))
                    then(dve.tensor_tensor(m2, m2, t2, ALU.max))
                    then(dve.tensor_tensor(m1, m1, m2, ALU.add))
                if parts == 1:
                    g = gtop[:, 0]
                    theirs = g.rearrange("p k (a i) -> p k a i", a=1).broadcast_to([P, TPC, N_GROUP, N_GROUP])
                    own = g.rearrange("p k (j a) -> p k j a", a=1).broadcast_to([P, TPC, N_GROUP, N_GROUP])
                    early = earlier[:].rearrange("p (a j) i -> p a j i", a=1).broadcast_to([P, TPC, N_GROUP, N_GROUP])
                    then(dve.tensor_tensor(ge4[:], theirs, own, ALU.is_ge))
                    then(dve.tensor_tensor(gt4[:], theirs, own, ALU.is_gt))
                    then(dve.tensor_tensor(ge4[:], ge4[:], early, ALU.mult))
                    then(dve.tensor_tensor(gt4[:], gt4[:], ge4[:], ALU.max))
                    then(dve.tensor_reduce(rank, gt4[:].rearrange("p k j i -> p (k j) i"), AX_X, ALU.add))
                    then(dve.tensor_scalar(t1, rank, 1.5, -BIG, ALU.is_ge, ALU.mult))
                    then(dve.tensor_tensor(masked[:].rearrange("p k (g e) -> p (k g) e", e=G8), grouped, over_e(t1), ALU.add), False)
                    wait_apart(dve, route_step, base + n[0], 6)
                    for k in range(TPC):
                        ins = dve.max(top8[:, k, :], masked[:, k, :])
                    then(ins, False)
                    wait_apart(dve, route_step, base + n[0], 7)
                    for k in range(TPC):
                        ins = dve.max_index(idx8[:, k, :], top8[:, k, :], masked[:, k, :])
                    then(ins)
                    then(dve.tensor_copy(idxf[:], idx8[:, :, 0:TOP_K]))
                if parts == 2:
                    for k in range(TPC):
                        ins = dve.tensor_tensor(chosen[:, k], iota_e[:].rearrange("p (a e) -> p a e", a=1).broadcast_to([P, TOP_K, E]),
                                                idxf[:, k].rearrange("p (i a) -> p i a", a=1).broadcast_to([P, TOP_K, E]), ALU.is_equal)
                    then(ins)
                    for k in range(TPC):
                        ins = dve.tensor_reduce(masked[:, k], chosen[:, k].rearrange("p i e -> p e i"), AX_X, ALU.add)
                    then(ins)
                    then(dve.tensor_tensor(masked[:], masked[:], sig[:], ALU.mult))
                    then(dve.tensor_reduce(wsum[:, 0], masked[:], AX_X, ALU.add))
                    then(dve.tensor_scalar(wsum[:, 1], wsum[:, 0], 1e-20, None, ALU.add))
                    then(dve.reciprocal(wsum[:, 0], wsum[:, 1]))
                    then(dve.tensor_scalar(wsum[:, 1], wsum[:, 0], ROUTED_SCALE, None, ALU.mult))
                    then(dve.tensor_tensor(cw[:, :, 0:E], masked[:], wsum[:, 1].rearrange("p (k a) -> p k a", a=1).broadcast_to([P, TPC, E]), ALU.mult))
                    then(dve.tensor_tensor(cw[:, :, E:RW], chosen[:, :, 0, 0:E:2], chosen[:, :, 0, 1:E:2], ALU.add))
                    then(dve.tensor_scalar(cw[:, :, E:RW], cw[:, :, E:RW], ANCHOR_ALPHA, None, ALU.mult))
                    then(dve.tensor_copy(cw_parts[:, :, 0:RW], cw[:]))
                    then(dve.tensor_tensor(cw_parts[:, :, RW:2 * RW], cw[:], cw_parts[:, :, 0:RW].bitcast(F32), ALU.subtract))
                assert n[0] == ROUTE_AT[parts + 1]

            def hidden(T, t, q):
                dve.wait_ge(silu_done, T + 1)
                dve.wait_ge(u_ps, T + 1)
                if not below(T, 3):
                    dve.wait_ge(hid_lo_done, T - 2)
                dve.tensor_tensor(prod_sb[:, q], pU[q][:], act_sb[:, q], ALU.mult).then_inc(au_done, 1)

            def weigh(T, t, q, c):
                dve.wait_ge(au_done, T + 1)
                if t == WT:
                    dve.tensor_copy(hid[:, t % 3], prod_sb[:, q]).then_inc(hid_done, 1)
                    return
                dve.wait_ge(c_ps, c * WT + (t + 1))
                dve.tensor_tensor(hid[:, t % 3], pC[t % 2][:], prod_sb[:, q], ALU.mult).then_inc(hid_done, 1)

            def result_out(c):
                dve.wait_ge(down_done, c * FT + FT)
                for s in range(SPC):
                    toks = slice(s * S, (s + 1) * S)
                    ins = dve.tensor_scalar(yT[:, toks], pY[:, toks], gbT[:, bass.ds(c * SPC + s, 1)], None, ALU.mult)
                ins.then_inc(yT_done, 1)

            def residual_out(c):
                dve.wait_ge(yT_ps, c + 1)
                t = x_all[:, bass.ds(c * TPC, TPC), :]
                dve.tensor_tensor(t, pM[:].rearrange("p (k d) -> p k d", k=TPC), t, ALU.add).then_inc(y_done, 1)

            dve.wait_ge(x_added, NB)
            layer_norm(0, 0)
            layer_norm(0, 1)
            input_out(0)
            for parts in range(3):
                route(0, parts)

            def chunk(c, par):
                first, last = isinstance(c, int) and c == 0, isinstance(c, int) and c == NCH - 1
                for t in range(FT):
                    q = (FT * par + t) % 2
                    T = c * FT + t
                    hidden(T, t, q)
                    weigh(T, t, q, c)
                    if t == 2 and not first:
                        result_out(c - 1)
                    if t == 4 and not first:
                        residual_out(c - 1)
                    if not last:
                        if t == 1:
                            layer_norm(c + 1, 0)
                        if t == 3:
                            layer_norm(c + 1, 1)
                        if t == 5:
                            input_out(c + 1)
                        if t in (11, 13, 15):
                            route(c + 1, (t - 11) // 2)

            each_chunk(dve, chunk)
            result_out(NCH - 1)
            residual_out(NCH - 1)

        ROUTE_AT = [0, 10, 20, 32]

        def prologue_dve(dve):
            steps, seen = [0], [0]

            def then(ins):
                steps[0] += 1
                ins.then_inc(pro_step, 1)
                dve.wait_ge(pro_step, steps[0])

            def bank():
                seen[0] += 1
                dve.wait_ge(pro_pe, seen[0])
                return banks[(seen[0] - 1) % 8]

            dve.tensor_copy(scT, bank()[:, 0:NB]).then_inc(pro_ev, 1)
            t = bank()
            then(dve.tensor_copy(gwT_hi[:], t[:, 0:E]))
            dve.tensor_tensor(gwT_lo[:], t[:, 0:E], gwT_hi[:].bitcast(F32), ALU.subtract).then_inc(pro_ev, 1)
            t = bank()
            dve.tensor_scalar(mod_rows[:, 0:D], t[0:NB, D:2 * D], 1.0, None, ALU.add).then_inc(mod_rows_made, 1)
            dve.tensor_copy(mod_rows[:, D:2 * D], t[0:NB, 0:D]).then_inc(mod_rows_made, 1)
            dve.wait_ge(mod_rows_made, 2)
            dve.engine_nop().then_inc(pro_ev, 1)
            t = bank()
            then(dve.tensor_copy(modT[:], t[:, 0:6 * NB].rearrange("p (m b) -> p m b", m=6)))
            dve.engine_nop().then_inc(pro_ev, 1)
            then(dve.tensor_scalar(modT[:, 4], modT[:, 4], 1.0, None, ALU.add))
            for m, dst in ((2, gaT), (5, gbT)):
                g = modT[:, m]
                then(dve.scalar_tensor_tensor(out=mod_tmp[:, 0], in0=g, scalar=-1.0, in1=g, op0=ALU.mult, op1=ALU.max))
                then(dve.tensor_scalar(mod_tmp[:, 0], mod_tmp[:, 0], 0.25, None, ALU.max))
                then(dve.tensor_scalar(mod_tmp[:, 1], g, 0.0, 2.0, ALU.is_ge, ALU.mult))
                then(dve.scalar_tensor_tensor(out=dst[:], in0=mod_tmp[:, 1], scalar=-1.0, in1=mod_tmp[:, 0], op0=ALU.add, op1=ALU.mult))
            for jj in range(0, PAIRS, 4):
                for ch in range(3):
                    t = bank()
                    if ch < 2:
                        hi = wqk_hi[:, ch, jj:jj + 4, :].rearrange("p j n -> p (j n)")
                        lo = wqk_lo[:, ch, jj:jj + 4, :].rearrange("p j n -> p (j n)")
                    else:
                        hi, lo = wv_hi[:, jj * P:(jj + 4) * P], wv_lo[:, jj * P:(jj + 4) * P]
                    sign = -1.0 if ch == 0 else 1.0
                    then(dve.tensor_scalar(hi, t[:], sign, None, ALU.mult))
                    dve.scalar_tensor_tensor(out=lo, in0=t[:], scalar=sign, in1=hi.bitcast(F32), op0=ALU.mult,
                                             op1=ALU.subtract).then_inc(pro_ev, 1)
            for jj in range(0, PAIRS, 4):
                dve.tensor_copy(woT[:, jj:jj + 4, :].rearrange("p j n -> p (j n)"), bank()[:]).then_inc(pro_ev, 1)
            dve.wait_ge(bias_loaded, 48)
            dve.tensor_scalar(nbq[:], bqkv[:, :, 0], -1.0, None, ALU.mult).then_inc(nbq_made, 1)
            for j in range(PAIRS + 1):
                if j < PAIRS:
                    dve.tensor_scalar(bv_diag[:, j % 2, :], ident[:], bqkv[:, j, 2:3], None, ALU.mult).then_inc(bv_diag_made, 1)
                if j:
                    dve.tensor_copy(bv_rows[:, (j - 1) * P:j * P], bank()[:, 0:P]).then_inc(pro_ev, 1)
            dve.wait_ge(pro_ev, 20)
            dve.wait_ge(nbq_made, 1)

        def split_weights(dve):
            for n in range(RAW_LOTS):
                hi, lo = raw_dst[n]
                dve.wait_ge(raw_loaded, 48 * (n + 1))
                dve.tensor_copy(hi, stage_gu).then_inc(raw_hi, 1)
                dve.wait_ge(raw_hi, n + 1)
                dve.tensor_tensor(lo, stage_gu, hi.bitcast(F32), ALU.subtract).then_inc(raw_lo, 1)

        @block.sync
        def _(sp):
            sp.dma_start(c_sb, cond).then_inc(mod_loaded, 16)
            sp.dma_start(wmod_sb, wmod).then_inc(mod_loaded, 16)
            sp.dma_start(gw_rows, gate_w).then_inc(mod_loaded, 16)
            sp.dma_start(x_all[:, 0:2 * KT, :], x[0:2].rearrange("b (k p) d -> p (b k) d", p=P)).then_inc(x_first, 16)
            sp.dma_start(wq_rows, W_qkv.rearrange("(j n c) i -> n j c i", n=P, c=3)).then_inc(w_loaded, 16)
            sp.dma_start(wo_rows, W_o).then_inc(w_loaded, 16)
            sp.dma_start(bqkv[:], b_qkv.rearrange("(j n c) -> n j c", n=P, c=3)).then_inc(bias_loaded, 16)
            sp.dma_start(bo_col[:], b_o.rearrange("(n a) -> n a", a=1)).then_inc(bias_loaded, 16)
            sp.dma_start(bias_row[:], gate_bias.rearrange("(a n) -> a n", a=1).broadcast_to([P, E])).then_inc(bias_loaded, 16)
            for b0 in range(2, NB, 10):
                sp.dma_start(x_all[:, b0 * KT:(b0 + 10) * KT, :],
                             x[b0:b0 + 10].rearrange("b (k p) d -> p (b k) d", p=P)).then_inc(x_loaded, 16)
            sp.wait_ge(mod_rows_made, 2)
            sp.dma_start(mod_dram, mod_rows).then_inc(mod_stored, 16)
            sp.wait_ge(mod_stored, 16)

            def mod_rows_load(b, par):
                sp.dma_start(mod_bc[:, par, :], mod_dram[bass.ds(b, 1), :].broadcast_to([P, 2 * D])).then_inc(mod_rows_in[par], 16)

            mod_rows_load(0, 0)
            mod_rows_load(1, 1)
            sp.wait_ge(pro_ev, 4)
            sp.wait_ge(consts_made, 7)
            for n in range(RAW_LOTS):
                if n:
                    sp.wait_ge(raw_lo, n)
                for dst, src in raw_lot(n):
                    sp.dma_start(dst, src).then_inc(raw_loaded, 16)

            with sp.Fori(1, NB // 2) as i:
                for k in range(2):
                    sp.wait_ge(hmod_step, i * 4 + (2 * k - 2))
                    mod_rows_load(i * 2 + k, k)

            out_v = out.rearrange("b (k p) d -> p (b k) d", p=P)
            with sp.Fori(0, NCH) as c:
                sp.wait_ge(y_done, c + 1)
                sp.dma_start(out_v[:, bass.ds(c * TPC, TPC), :], x_all[:, bass.ds(c * TPC, TPC), :]).then_inc(y_stored, 16)
            sp.wait_ge(y_stored, 16 * NCH)

        @block.gpsimd
        def _(pool):
            pool.memset(ones[:], 1.0).then_inc(consts_made, 1)
            pool.memset(ident[:], 0.0).then_inc(pick_made, 1)
            pool.memset(causal[:], 0.0).then_inc(pick_made, 1)
            pool.memset(half_pow[:], -0.5).then_inc(consts_made, 1)
            pool.memset(earlier[:], 1.0).then_inc(pick_made, 1)
            pool.wait_ge(pick_made, 3)
            pool.affine_select(out=ident[:], in_=ident[:], compare_op=ALU.not_equal, fill=1.0, base=0,
                               pattern=[[-1, P]], channel_multiplier=1).then_inc(consts_made, 1)
            pool.affine_select(out=causal[:, 0:S], in_=causal[:, 0:S], compare_op=ALU.is_ge, fill=BIG, base=0,
                               pattern=[[1, S]], channel_multiplier=-1)
            pool.affine_select(out=causal[:, S:SW], in_=causal[:, S:SW], compare_op=ALU.is_ge, fill=BIG, base=0,
                               pattern=[[1, P]], channel_multiplier=-1).then_inc(consts_made, 1)
            pool.affine_select(out=earlier[:], in_=earlier[:], compare_op=ALU.is_ge, fill=0.0, base=-1,
                               pattern=[[1, N_GROUP], [-1, N_GROUP]], channel_multiplier=0).then_inc(consts_made, 1)
            pool.iota(iota_e[:], pattern=[[1, E]], base=0, channel_multiplier=0,
                      allow_small_or_imprecise_dtypes=True).then_inc(consts_made, 1)
            pool.memset(stage[:, WT * P:FT * P], 0.0).then_inc(consts_made, 1)

            def rstd_of(b, par):
                pool.wait_ge(norm_step, b * NORM_STEPS + 5)
                pool.tensor_tensor(rstd[:, 0:KT], var_eps[:, 0:KT], half_pow[:, 0:KT], ALU.pow).then_inc(pow_done, 1)

            def modulate(b, par):
                pool.wait_ge(norm_step, b * NORM_STEPS + 7)
                pool.wait_ge(mod_rows_in[par], b * 8 + (16 - 8 * par))
                m = mod_bc[:, par, :].rearrange("p (a k d) -> p a k d", a=2, k=1)
                pool.tensor_tensor(hmul[:], xhat[:, 0:KT, :], m[:, 0].broadcast_to([P, KT, D]), ALU.mult).then_inc(hmod_step, 1)
                pool.wait_ge(hmod_step, b * 2 + 1)
                pool.tensor_tensor(hmod[:], hmul[:], m[:, 1].broadcast_to([P, KT, D]), ALU.add).then_inc(hmod_step, 1)

            def rrms_of(b, par):
                pool.wait_ge(norm_step, b * NORM_STEPS + 10)
                pool.tensor_tensor(rrms[:], ms_eps[:], half_pow[:, 0:KT], ALU.pow).then_inc(pow_done, 1)

            def scale_v(g, j, par, v_need):
                pool.wait_ge(rz_done, g + 1)
                pool.wait_ge(v_done, v_need)
                if not (isinstance(g, int) and g < 2):
                    pool.wait_ge(z_ps, g - 1)
                pool.tensor_tensor(
                    vn[:, j % 2].rearrange("p k (h d) -> p k h d", d=DH),
                    v_sb[:, par, :, j * P:(j + 1) * P].rearrange("p k (h d) -> p k h d", d=DH),
                    rz[:, j % 2].rearrange("p k (h a) -> p k h a", a=1).broadcast_to([P, KT, 2, DH]),
                    ALU.mult).then_inc(vn_done, 1)

            rstd_of(0, 0)
            modulate(0, 0)
            rrms_of(0, 0)
            pool.memset(pick[:].bitcast(F32), 0.0).then_inc(pick_made, 1)
            pool.wait_ge(pick_made, 4)
            for n, (t0, nt, first, per) in enumerate(((0, ET, 0, P // EI), (ET, AT, E, P // AI))):
                v = pick[:, t0:t0 + nt, :].rearrange("p t (w n) -> p t w n", w=per)
                for part in range(2):
                    pool.affine_select(out=v, in_=v, compare_op=ALU.not_equal, fill=1.0, base=-first - part * RW,
                                       pattern=[[-per, nt], [-1, per], [0, P // per]],
                                       channel_multiplier=1).then_inc(pick_made, 1)
                    pool.wait_ge(pick_made, 5 + 2 * n + part)

            def sequence(b, par):
                for j in range(PAIRS):
                    if j:
                        scale_v(b * PAIRS + (j - 1), j - 1, par, b * 4 + (2 if j <= PAIRS // 2 else 4))
                    elif not is_first(b):
                        scale_v(b * PAIRS - 1, PAIRS - 1, 1 - par, b * 4)
                    if not is_last(b):
                        if j == 0:
                            rstd_of(b + 1, 1 - par)
                        if j == 1:
                            modulate(b + 1, 1 - par)
                        if j == 2:
                            rrms_of(b + 1, 1 - par)

            each_sequence(pool, sequence)
            scale_v(NB * PAIRS - 1, PAIRS - 1, 1, NB * 4)

            ffn_pool(pool)

        def three(pe, dst, lhs_hi, lhs_lo, rhs_hi, rhs_lo, start=True, stop=True):
            pe.matmul(dst, lhs_hi, rhs_hi, start=start, stop=False)
            pe.matmul(dst, lhs_hi, rhs_lo, start=False, stop=False)
            return pe.matmul(dst, lhs_lo, rhs_hi, start=False, stop=stop)

        def prologue_pe(pe):
            n = [0]

            def bank():
                if n[0] >= 8:
                    pe.wait_ge(pro_ev, n[0] - 7)
                n[0] += 1
                return banks[(n[0] - 1) % 8]

            pe.wait_ge(consts_made, 7)
            pe.wait_ge(silu_c_done, 1)
            pe.transpose(bank()[:, 0:NB], sc_sb, ident[0:NB, 0:NB]).then_inc(pro_pe, 1)
            pe.wait_ge(mod_loaded, 48)
            pe.transpose(bank()[:, 0:E], gw_rows, ident[0:E, 0:E]).then_inc(pro_pe, 1)
            pe.wait_ge(pro_ev, 1)
            t = bank()
            pe.matmul(t[0:NB, 0:2 * D], scT, wmod_sb[:, 0:2 * D], start=True, stop=True).then_inc(pro_pe, 1)
            t = bank()
            for m in range(6):
                ins = pe.matmul(t[:, m * NB:(m + 1) * NB], wmod_sb[:, m * D:(m + 1) * D], scT, start=True, stop=True)
            ins.then_inc(pro_pe, 1)
            pe.wait_ge(w_loaded, 32)
            for jj in range(0, PAIRS, 4):
                for c in range(3):
                    t = bank()
                    for k in range(4):
                        ins = pe.transpose(t[:, k * P:(k + 1) * P], wq_rows[:, jj + k, c, :], ident[:])
                    ins.then_inc(pro_pe, 1)
            for jj in range(0, PAIRS, 4):
                t = bank()
                for k in range(4):
                    ins = pe.transpose(t[:, k * P:(k + 1) * P], wo_rows[:, (jj + k) * P:(jj + k + 1) * P], ident[:])
                ins.then_inc(pro_pe, 1)
            for j in range(PAIRS):
                pe.wait_ge(bv_diag_made, j + 1)
                pe.matmul(bank()[:, 0:P], ones[:], bv_diag[:, j % 2, :], start=True, stop=True).then_inc(pro_pe, 1)
            pe.wait_ge(pro_ev, n[0])

        def transpose_normed(pe, b):
            pe.wait_ge(norm_step, b * NORM_STEPS + NORM_STEPS)
            for k in range(KT):
                ins = pe.transpose(pM[:, k * P:(k + 1) * P], normed[:, k, :], ident[:])
            ins.then_inc(nT_ps, 1)

        def values(pe, b, par, chunk):
            half, k = chunk // 2, chunk % 2
            if chunk == 0:
                pe.wait_ge(nT_hi_done, b + 1)
                pe.wait_ge(nT_lo_done, b + 1)
            if not (isinstance(b, int) and b == 0 and chunk == 0):
                pe.wait_ge(v_done, b * 4 + chunk)
            toks = slice(k * P, (k + 1) * P)
            cols = slice(half * 512, (half + 1) * 512)
            three(pe, pM[:], nT_hi[:, par, toks], nT_lo[:, par, toks], wv_hi[:, cols], wv_lo[:, cols]).then_inc(v_ps, 1)

        def project(pe, g, j, par):
            if not (isinstance(g, int) and g < 2):
                pe.wait_ge(qk_lo_done, g - 1)
            for w in range(2):
                ins = three(pe, pQK[j % 2][:, w * S:(w + 1) * S], wqk_hi[:, w, j, :], wqk_lo[:, w, j, :],
                            nT_hi[:, par], nT_lo[:, par])
            ins.then_inc(qk_ps, 1)

        def scores(pe, g, j):
            pe.wait_ge(qk_lo_done, g + 1)
            for h in range(2):
                if not (isinstance(g, int) and g < 2):
                    pe.wait_ge(s_masked, g * 2 + (h - 3))
                r = slice(h * DH, (h + 1) * DH)
                t = pS[(2 * j + h) % 4]
                for k in range(KT):
                    keys = slice(k * P, (k + 1) * P)
                    dst = t[:, 0:S] if k == 0 else t[:, S:SW]
                    ins = three(pe, dst, qk_hi[r, j % 2, 1, keys], qk_lo[r, j % 2, 1, keys],
                                qk_hi[r, j % 2, 0, k * P:S], qk_lo[r, j % 2, 0, k * P:S])
                ins.then_inc(s_ps, 1)

        def attend(pe, g, j):
            pe.wait_ge(e_done, g * 2 + 2)
            pe.wait_ge(vn_done, g + 1)
            if not (isinstance(g, int) and g == 0):
                pe.wait_ge(z_done, g)
            for k in range(KT):
                for h in range(2):
                    src = s_sb[:, (2 * j + h) % 4, :]
                    ins = pe.matmul(pZ[h * DH:(h + 1) * DH, k * P:S], vn[:, j % 2, k, h * DH:(h + 1) * DH],
                                    src[:, 0:S] if k == 0 else src[:, S:SW], start=(k == 0), stop=(k == KT - 1))
            ins.then_inc(z_ps, 1)

        def out_projection(pe, b, par):
            pe.wait_ge(z_done, b * PAIRS + PAIRS)
            if is_last(b):
                pe.wait_ge(x_added, last_b)
            else:
                pe.wait_ge(v_done, b * 4 + 8)
            for j in range(PAIRS):
                ins = pe.matmul(pM[:, 0:S], woT[:, j, :], zT[:, par, j, :], start=(j == 0), stop=(j == PAIRS - 1))
            ins.then_inc(o_ps, 1)

        def transpose_att(pe, b):
            pe.wait_ge(att_done, b + 1)
            for k in range(KT):
                ins = pe.transpose(pM[:, k * P:(k + 1) * P], attT[:, k * P:(k + 1) * P], ident[:])
            ins.then_inc(attT_ps, 1)

        @block.tensor
        def _(pe):
            prologue_pe(pe)
            transpose_normed(pe, 0)
            for chunk in range(3):
                values(pe, 0, 0, chunk)
            project(pe, 0, 0, 0)

            def sequence(b, par):
                for j in range(PAIRS):
                    g = b * PAIRS + j
                    if j == PAIRS - 1:
                        if not is_last(b):
                            project(pe, g + 1, 0, 1 - par)
                    else:
                        project(pe, g + 1, j + 1, par)
                    scores(pe, g, j)
                    if j == 0:
                        values(pe, b, par, 3)
                    if j == 2 and not is_first(b):
                        out_projection(pe, b - 1, 1 - par)
                    if j == 3 and not is_first(b):
                        transpose_att(pe, b - 1)
                    if j == 4 and not is_last(b):
                        if is_first(b):
                            pe.wait_ge(v_done, 4)
                        else:
                            pe.wait_ge(x_added, b)
                        transpose_normed(pe, b + 1)
                    if j >= 5 and not is_last(b):
                        values(pe, b + 1, 1 - par, j - 5)
                    if j:
                        attend(pe, g - 1, j - 1)
                    elif not is_first(b):
                        attend(pe, g - 1, PAIRS - 1)

            each_sequence(pe, sequence)
            attend(pe, NB * PAIRS - 1, PAIRS - 1)
            out_projection(pe, last_b, 1)
            transpose_att(pe, last_b)
            ffn_tensor(pe)

        @block.scalar
        def _(act):
            act.wait_ge(mod_loaded, 48)
            act.activation(sc_sb, c_sb, ACT.Silu).then_inc(silu_c_done, 1)

            def normed_hi(b, par):
                act.wait_ge(nT_ps, b + 1)
                act.activation(nT_hi[:, par], pM[:, 0:S], ACT.Copy).then_inc(nT_hi_done, 1)

            def qk_high(g, j):
                act.wait_ge(qk_ps, g + 1)
                if not (isinstance(g, int) and g < 2):
                    act.wait_ge(s_ps, g * 2 - 2)
                act.activation(qk_hi[:, j % 2, 0], pQK[j % 2][:, 0:S], ACT.Identity, bias=nbq[:, j:j + 1])
                act.activation(qk_hi[:, j % 2, 1], pQK[j % 2][:, S:2 * S], ACT.Identity,
                               bias=bqkv[:, j, 1:2]).then_inc(qk_hi_done, 1)

            def exponentials(g, j):
                if not (isinstance(g, int) and g < 2):
                    act.wait_ge(rz_done, g - 1)
                for h in range(2):
                    act.wait_ge(s_masked, g * 2 + (h + 1))
                    n = (2 * j + h) % 4
                    for k in range(KT):
                        cols = slice(0, S) if k == 0 else slice(S, SW)
                        ins = act.activation(s_sb[:, n, cols], s_sb[:, n, cols], ACT.Exp, bias=smin[:, n, k:k + 1],
                                             scale=-1.0, accum_out=zsum[:, j % 2, k, h:h + 1])
                    ins.then_inc(e_done, 1)

            def z_out(g, j, par, b):
                act.wait_ge(z_ps, g + 1)
                if j == 0 and not (isinstance(b, int) and b < 2):
                    act.wait_ge(o_ps, b - 1)
                act.activation(zT[:, par, j, :], pZ[:, 0:S], ACT.Copy).then_inc(z_done, 1)

            normed_hi(0, 0)
            act.wait_ge(nbq_made, 1)
            act.wait_ge(bias_loaded, 48)
            qk_high(0, 0)

            def sequence(b, par):
                for j in range(PAIRS):
                    g = b * PAIRS + j
                    if not (is_last(b) and j == PAIRS - 1):
                        qk_high(g + 1, (j + 1) % PAIRS)
                    if j >= 2:
                        z_out(g - 2, j - 2, par, b)
                    elif not is_first(b):
                        z_out(g - 2, j - 2 + PAIRS, 1 - par, b - 1)
                    exponentials(g, j)
                    if j == 4 and not is_last(b):
                        normed_hi(b + 1, 1 - par)

            each_sequence(act, sequence)
            z_out(NB * PAIRS - 2, PAIRS - 2, 1, last_b)
            z_out(NB * PAIRS - 1, PAIRS - 1, 1, last_b)
            ffn_scalar(act)

        @block.vector
        def _(dve):
            prologue_dve(dve)

            def norm(b, par, stage_no):
                base = b * NORM_STEPS
                tiles = [b * KT + k for k in range(KT)]

                def xt(k):
                    return x_all[:, bass.ds(tiles[k], 1), :].rearrange("p a d -> p (a d)")

                if stage_no == 0:
                    for k in range(KT):
                        dve.bn_stats(bnst[:, k, :], xt(k)).then_inc(norm_step, 1)
                    wait_apart(dve, norm_step, base + 2, 4)
                    for k in range(KT):
                        dve.bn_aggr(mv[:, k, :], bnst[:, k, :]).then_inc(norm_step, 1)
                    dve.wait_ge(norm_step, base + 4)
                    dve.tensor_scalar(var_eps[:, 0:KT], mv[:, 0:KT, 1], LN_EPS, None, ALU.add).then_inc(norm_step, 1)
                if stage_no == 1:
                    dve.wait_ge(pow_done, b * 2 + 1)
                    for k in range(KT):
                        dve.tensor_scalar(xhat[:, k, :], xt(k), mv[:, k, 0:1], rstd[:, k:k + 1],
                                          ALU.subtract, ALU.mult).then_inc(norm_step, 1)
                if stage_no == 2:
                    dve.wait_ge(hmod_step, b * 2 + 2)
                    for k in range(KT):
                        dve.tensor_tensor_reduce(sq_junk[:, k, :], hmod[:, k, :], hmod[:, k, :], 1.0, 0.0, ALU.mult,
                                                 ALU.add, sumsq[:, k:k + 1]).then_inc(norm_step, 1)
                    dve.wait_ge(norm_step, base + 9)
                    dve.tensor_scalar(ms_eps[:], sumsq[:], 1.0 / D, RMS_EPS, ALU.mult, ALU.add).then_inc(norm_step, 1)
                if stage_no == 3:
                    dve.wait_ge(pow_done, b * 2 + 2)
                    for k in range(KT):
                        dve.tensor_scalar(normed[:, k, :], hmod[:, k, :], rrms[:, k:k + 1], None,
                                          ALU.mult).then_inc(norm_step, 1)

            def normed_lo(b, par):
                dve.wait_ge(nT_hi_done, b + 1)
                dve.tensor_tensor(nT_lo[:, par], pM[:, 0:S], nT_hi[:, par].bitcast(F32), ALU.subtract).then_inc(nT_lo_done, 1)

            def value_rows(b, par, chunk):
                half, k = chunk // 2, chunk % 2
                dve.wait_ge(v_ps, b * 4 + (chunk + 1))
                cols = slice(half * 512, (half + 1) * 512)
                dve.tensor_tensor(v_sb[:, par, k, cols], pM[:], bv_rows[:, cols], ALU.add).then_inc(v_done, 1)

            def qk_low(g, j):
                dve.wait_ge(qk_hi_done, g + 1)
                bias = (nbq[:, j:j + 1], bqkv[:, j, 1:2])
                for w in range(2):
                    ins = dve.scalar_tensor_tensor(out=qk_lo[:, j % 2, w], in0=pQK[j % 2][:, w * S:(w + 1) * S],
                                                   scalar=bias[w], in1=qk_hi[:, j % 2, w].bitcast(F32),
                                                   op0=ALU.add, op1=ALU.subtract)
                ins.then_inc(qk_lo_done, 1)

            def sums(g, j):
                dve.wait_ge(e_done, g * 2 + 2)
                dve.reciprocal(rz[:, j % 2], zsum[:, j % 2]).then_inc(rz_done, 1)

            def mask_and_min(g, j):
                for h in range(2):
                    n = (2 * j + h) % 4
                    if not (isinstance(g, int) and g < 2):
                        dve.wait_ge(z_ps, g - 1)
                    wait_apart(dve, s_ps, g * 2 + (h + 1), n)
                    for k in range(KT):
                        cols = slice(0, S) if k == 0 else slice(S, SW)
                        ins = dve.tensor_tensor_reduce(s_sb[:, n, cols], pS[n][:, cols], causal[:, cols], 1.0, 3e38,
                                                       ALU.add, ALU.min, smin[:, n, k:k + 1])
                    ins.then_inc(s_masked, 1)

            def att_out(b):
                dve.wait_ge(o_ps, b + 1)
                dve.tensor_scalar(attT[:], pM[:, 0:S], bo_col[:, 0:1], gaT[:, bass.ds(b, 1)], ALU.add, ALU.mult).then_inc(att_done, 1)

            def residual(b):
                dve.wait_ge(attT_ps, b + 1)
                t = x_all[:, bass.ds(b * KT, KT), :]
                dve.tensor_tensor(t, pM[:, 0:S].rearrange("p (k d) -> p k d", k=KT), t, ALU.add).then_inc(x_added, 1)

            dve.wait_ge(x_first, 16)
            for st in range(4):
                norm(0, 0, st)
            normed_lo(0, 0)
            for chunk in range(3):
                value_rows(0, 0, chunk)
            qk_low(0, 0)
            split_weights(dve)
            dve.wait_ge(x_loaded, 48)

            def sequence(b, par):
                for j in range(PAIRS):
                    g = b * PAIRS + j
                    if not (is_last(b) and j == PAIRS - 1):
                        qk_low(g + 1, (j + 1) % PAIRS)
                    if j:
                        sums(g - 1, j - 1)
                    elif not is_first(b):
                        sums(g - 1, PAIRS - 1)
                    mask_and_min(g, j)
                    if j == 0:
                        value_rows(b, par, 3)
                    if j < 4 and not is_last(b):
                        norm(b + 1, 1 - par, j)
                    if j == 2 and not is_first(b):
                        att_out(b - 1)
                    if j == 3 and not is_first(b):
                        residual(b - 1)
                    if j == 4 and not is_last(b):
                        normed_lo(b + 1, 1 - par)
                    if j >= 5 and not is_last(b):
                        value_rows(b + 1, 1 - par, j - 5)

            each_sequence(dve, sequence)
            sums(NB * PAIRS - 1, PAIRS - 1)
            att_out(last_b)
            residual(last_b)
            ffn_vector(dve)



_INS = ['L0_attn_x', 'L0_attn_W_qkv', 'L0_attn_b_qkv', 'L0_attn_W_o', 'L0_attn_b_o', 'L0_ffn_gate_weight',
        'L0_ffn_gate_bias', 'L0_ffn_w_gate', 'L0_ffn_w_up', 'L0_ffn_w_down', 'L0_ffn_shared_w_gate',
        'L0_ffn_shared_w_up', 'L0_ffn_shared_w_down', 'L0_ffn_anchor_w_gate', 'L0_ffn_anchor_w_up',
        'L0_ffn_anchor_w_down', 'L0_c', 'L0_wmod']


def kernel(**inputs):
    import numpy as _np
    import concourse.bacc as _bacc
    from concourse import mybir as _mybir
    from concourse.bass_utils import run_bass_kernel_spmd as _run

    nc = _bacc.Bacc("TRN2", target_bir_lowering=False, num_devices=1)
    arrays, args = {}, []
    for name in _INS:
        a = _np.ascontiguousarray(inputs[name])
        arrays[f"in_{name}_dram"] = a
        args.append(nc.dram_tensor(f"in_{name}_dram", a.shape, _mybir.dt.from_np(a.dtype), kind="ExternalInput").ap())
    shape = inputs['L0_attn_x'].shape
    args.append(nc.dram_tensor("out_0_dram", shape, _mybir.dt.float32, kind="ExternalOutput").ap())
    adaln_block_kernel(nc, *args)
    r = _run(nc, [arrays], core_ids=[0])
    return r.results[0]["out_0_dram"]
```

```python
from contextlib import ExitStack

import concourse.bass as bass
from concourse import mybir

ALU = mybir.AluOpType
ACT = mybir.ActivationFunctionType
F32 = mybir.dt.float32
F32R = mybir.dt.float32r
U32 = mybir.dt.uint32
AX_X = mybir.AxisListType.X

P = 128
LN_EPS = 1e-05
RMS_EPS = 1.1920929e-07
ROUTED_SCALE = 0.2
ANCHOR_ALPHA = 0.1
TOP_K = 6
N_GROUP = 4
BIG = 1e30


def adaln_block_kernel(nc, x, W_qkv, b_qkv, W_o, b_o, gate_w, gate_bias, w_gate, w_up, w_down,
                       sh_gate, sh_up, sh_down, an_gate, an_up, an_down, cond, wmod, out):
    NB, S, D = x.shape
    KT = S // P
    HD = W_o.shape[1]
    DH = 64
    PAIRS = HD // P
    E, _, EI = w_gate.shape
    L, _, AI = an_gate.shape
    ET = E * EI // P
    AT = L * AI // P
    WT = ET + AT
    FT = WT + 1
    SW = S + P
    CH = 512
    NCH = NB * S // CH
    TPC = CH // P
    SPC = CH // S
    RW = E + L
    NORM_STEPS = 12

    mod_dram = nc.dram_tensor("mod_rows", (NB, 2 * D), F32, kind="Internal").ap()

    with ExitStack() as ctx:
        memory = ctx

        def sb(name, shape, dt=F32):
            return memory.enter_context(nc.sbuf_tensor(name, shape, dt))

        def pb(name):
            return ctx.enter_context(nc.psum_tensor(name, [P, 512], F32))

        def sem(name):
            return ctx.enter_context(nc.semaphore(name))

        ident = sb("ident", [P, P])
        ones = sb("ones", [P, P])
        causal = sb("causal", [P, SW])
        earlier = sb("earlier", [P, N_GROUP, N_GROUP])
        iota_e = sb("iota_e", [P, E])
        unused = sb("unused", [P, 8])
        half_pow = sb("half_pow", [P, TPC])
        pick = sb("pick", [P, WT, P], F32R)
        wqk_hi = sb("wqk_hi", [P, 2, PAIRS, P], F32R)
        wqk_lo = sb("wqk_lo", [P, 2, PAIRS, P], F32R)
        wv_hi = sb("wv_hi", [P, HD], F32R)
        wv_lo = sb("wv_lo", [P, HD], F32R)
        woT_hi = sb("woT_hi", [P, PAIRS, D], F32R)
        woT_lo = sb("woT_lo", [P, PAIRS, D], F32R)
        bqkv = sb("bqkv", [P, PAIRS, 3])
        nbq = sb("nbq", [P, PAIRS])
        bv_diag = sb("bv_diag", [P, 2, P])
        bv_rows = sb("bv_rows", [P, HD])
        bo_col = sb("bo_col", [P, 1])
        bias_row = sb("bias_row", [P, E])
        wgu_hi = sb("wgu_hi", [P, 2, FT, P], F32R)
        wgu_lo = sb("wgu_lo", [P, 2, FT, P], F32R)
        wd_hi = sb("wd_hi", [P, FT, D], F32R)
        wd_lo = sb("wd_lo", [P, FT, D], F32R)
        gwT_hi = sb("gwT_hi", [P, E], F32R)
        gwT_lo = sb("gwT_lo", [P, E], F32R)
        modT = sb("modT", [P, 6, NB])
        mod_tmp = sb("mod_tmp", [P, 2, NB])
        gaT = sb("gaT", [P, NB])
        gbT = sb("gbT", [P, NB])
        x_all = sb("x_all", [P, NB * KT, D])

        memory = ExitStack()
        bnst = sb("bnst", [P, TPC, 6])
        mv = sb("mv", [P, TPC, 2])
        var_eps = sb("var_eps", [P, TPC])
        rstd = sb("rstd", [P, TPC])
        sumsq = sb("sumsq", [P, KT])
        ms_eps = sb("ms_eps", [P, KT])
        rrms = sb("rrms", [P, KT])
        sq_junk = sb("sq_junk", [P, KT, D])
        xhat = sb("xhat", [P, TPC, D])
        hmod = sb("hmod", [P, KT, D])
        hmul = sb("hmul", [P, KT, D])
        normed = sb("normed", [P, KT, D])
        mod_bc = sb("mod_bc", [P, 2, 2 * D])
        nT_hi = sb("nT_hi", [P, 2, S], F32R)
        nT_lo = sb("nT_lo", [P, 2, S], F32R)
        qk_hi = sb("qk_hi", [P, 2, 2, S], F32R)
        qk_lo = sb("qk_lo", [P, 2, 2, S], F32R)
        v_sb = sb("v_sb", [P, 2, KT, HD])
        vn = sb("vn", [P, 2, KT, P])
        s_sb = sb("s_sb", [P, 4, SW])
        smin = sb("smin", [P, 4, KT])
        zsum = sb("zsum", [P, 2, KT, 2])
        rz = sb("rz", [P, 2, KT, 2])
        zT_hi = sb("zT_hi", [P, 2, S], F32R)
        zT_lo = sb("zT_lo", [P, 2, S], F32R)
        stage = sb("stage", [P, FT * P])
        attT = sb("attT", [P, S])

        memory.close()
        memory = ctx

        mv2 = sb("mv2", [P, TPC, 2])
        bnst2 = sb("bnst2", [P, TPC, 6])
        var_eps2 = sb("var_eps2", [P, TPC])
        rstd2 = sb("rstd2", [P, TPC])
        xhat2 = sb("xhat2", [P, TPC, D])
        hT = sb("hT", [P, CH])
        hT_hi = sb("hT_hi", [P, 2, CH], F32R)
        hT_lo = sb("hT_lo", [P, 2, CH], F32R)
        sig = sb("sig", [P, TPC, E])
        sel = sb("sel", [P, TPC, E])
        dup = sb("dup", [P, TPC * N_GROUP, E // N_GROUP])
        masked = sb("masked", [P, TPC, E])
        gtop = sb("gtop", [P, 6, TPC, N_GROUP])
        ge4 = sb("ge4", [P, TPC, N_GROUP, N_GROUP])
        gt4 = sb("gt4", [P, TPC, N_GROUP, N_GROUP])
        top8 = sb("top8", [P, TPC, 8])
        idx8 = sb("idx8", [P, TPC, 8], U32)
        idxf = sb("idxf", [P, TPC, TOP_K])
        chosen = sb("chosen", [P, TPC, TOP_K, E])
        cw = sb("cw", [P, TPC, RW])
        wsum = sb("wsum", [P, 2, TPC])
        cw_parts = sb("cw_parts", [P, TPC, 2 * RW], F32R)
        cwT = sb("cwT", [2 * RW, 2, CH], F32R)
        act_sb = sb("act_sb", [P, 2, CH])
        prod_sb = sb("prod_sb", [P, 2, CH])
        hid = sb("hid", [P, 3, CH])
        hid_hi = sb("hid_hi", [P, 3, CH], F32R)
        hid_lo = sb("hid_lo", [P, 3, CH], F32R)
        yT = sb("yT", [P, CH])

        banks = [pb(f"bank{i}") for i in range(8)]
        pQK, pS, pZ, pO, pM = banks[0:2], banks[2:4], banks[4], banks[5], banks[6:8]

        x_first = sem("x_first")
        x_loaded = sem("x_loaded")
        w_loaded = sem("w_loaded")
        mod_loaded = sem("mod_loaded")
        bias_loaded = sem("bias_loaded")
        consts_made = sem("consts_made")
        pick_made = sem("pick_made")
        silu_c_done = sem("silu_c_done")
        pro_pe = sem("pro_pe")
        pro_ev = sem("pro_ev")
        pro_step = sem("pro_step")
        mod_rows_made = sem("mod_rows_made")
        nbq_made = sem("nbq_made")
        bv_diag_made = sem("bv_diag_made")
        mod_stored = sem("mod_stored")
        raw_loaded = sem("raw_loaded")
        raw_hi = sem("raw_hi")
        raw_lo = sem("raw_lo")
        mod_rows_in = [sem(f"mod_rows_in{i}") for i in range(2)]
        norm_step = sem("norm_step")
        pow_done = sem("pow_done")
        hmod_step = sem("hmod_step")
        nT_ps = sem("nT_ps")
        nT_hi_done = sem("nT_hi_done")
        nT_lo_done = sem("nT_lo_done")
        qk_ps = sem("qk_ps")
        qk_hi_done = sem("qk_hi_done")
        qk_lo_done = sem("qk_lo_done")
        s_ps = sem("s_ps")
        s_masked = sem("s_masked")
        e_done = sem("e_done")
        rz_done = sem("rz_done")
        vn_done = sem("vn_done")
        v_ps = sem("v_ps")
        v_done = sem("v_done")
        z_ps = sem("z_ps")
        z_hi_done = sem("z_hi_done")
        z_lo_done = sem("z_lo_done")
        o_ps = sem("o_ps")
        att_done = sem("att_done")
        attT_ps = sem("attT_ps")
        x_added = sem("x_added")
        ln_step = sem("ln_step")
        pow2_done = sem("pow2_done")
        xT_ps = sem("xT_ps")
        hT_done = sem("hT_done")
        hT_hi_done = sem("hT_hi_done")
        hT_lo_done = sem("hT_lo_done")
        logit_ps = sem("logit_ps")
        sig_done = sem("sig_done")
        route_step = sem("route_step")
        cwT_ps = sem("cwT_ps")
        cwT_done = sem("cwT_done")
        g_ps = sem("g_ps")
        u_ps = sem("u_ps")
        c_ps = sem("c_ps")
        silu_done = sem("silu_done")
        au_done = sem("au_done")
        hid_done = sem("hid_done")
        hid_hi_done = sem("hid_hi_done")
        hid_lo_done = sem("hid_lo_done")
        down_done = sem("down_done")
        yT_done = sem("yT_done")
        yT_ps = sem("yT_ps")
        y_done = sem("y_done")
        y_stored = sem("y_stored")

        wq_rows = v_sb[:].rearrange("p a k n -> p (a k n)")[:, 0:PAIRS * 3 * P].rearrange(
            "p (j c i) -> p j c i", j=PAIRS, c=3)
        wo_rows = v_sb[:].rearrange("p a k n -> p (a k n)")[:, PAIRS * 3 * P:PAIRS * 4 * P]
        wmod_sb = stage[:, 0:6 * D]
        c_sb = stage[0:NB, 6 * D:7 * D]
        sc_sb = stage[0:NB, 7 * D:8 * D]
        gw_rows = stage[0:E, 8 * D:9 * D]
        scT = stage[:, 9 * D:9 * D + NB]
        mod_rows = stage[0:NB, 10 * D:12 * D]
        stage_gu = stage[:].rearrange("p (t n) -> p t n", n=P)

        def raw_lot(n):
            if n < 2:
                w, a, s = ((w_gate, an_gate, sh_gate), (w_up, an_up, sh_up))[n]
                return [
                    (stage[:, 0:ET * P].rearrange("p (e i) -> p e i", i=EI), w.rearrange("e h i -> h e i")),
                    (stage[:, ET * P:WT * P].rearrange("p (l i) -> p l i", i=AI), a.rearrange("l h i -> h l i")),
                    (stage[:, WT * P:WT * P + EI], s),
                ]
            return [
                (stage_gu[:, 0:ET, :], w_down.rearrange("(t e) i h -> (e i) t h", e=P // EI)),
                (stage_gu[:, ET:WT, :], an_down.rearrange("(t l) i h -> (l i) t h", l=P // AI)),
                (stage_gu[0:EI, WT, :], sh_down),
            ]

        RAW_LOTS = 3
        PIECE = 3
        PIECES = FT // PIECE
        assert PIECES * PIECE == FT

        def raw_piece(n):
            lot, tiles = n // PIECES, slice(n % PIECES * PIECE, (n % PIECES + 1) * PIECE)
            hi, lo = (wd_hi[:], wd_lo[:]) if lot == 2 else (wgu_hi[:, lot], wgu_lo[:, lot])
            return stage_gu[:, tiles, :], hi[:, tiles, :], lo[:, tiles, :]

        def raw_pieces(g):
            if not isinstance(g, int):
                return ()
            lot, k = g // 5, g % 5
            return range(lot * PIECES + 2 * k, lot * PIECES + min(2 * k + 2, PIECES)) if lot < RAW_LOTS else ()

        block = ctx.enter_context(nc.Block())
        last_b = NB - 1

        def each_sequence(eng, body):
            body(0, 0)
            body(1, 1)
            with eng.Fori(1, NB // 2 - 1) as i:
                body(i * 2, 0)
                body(i * 2 + 1, 1)
            body(NB - 2, 0)
            body(NB - 1, 1)

        def is_first(b):
            return isinstance(b, int) and b == 0

        def is_last(b):
            return isinstance(b, int) and b == last_b

        def each_chunk(eng, body):
            body(0, 0)
            body(1, 1)
            with eng.Fori(1, NCH // 2 - 1) as i:
                body(i * 2, 0)
                body(i * 2 + 1, 1)
            body(NCH - 2, 0)
            body(NCH - 1, 1)

        def wait_apart(eng, semaphore, count, cell):
            eng.wait_ge(semaphore, count)
            if not isinstance(count, int):
                eng.memset(unused[:, cell:cell + 1], 0.0)

        def below(n, limit):
            return isinstance(n, int) and n < limit


        pG, pU, pC, pY, pX = banks[0:2], banks[2:4], banks[4:6], banks[6], banks[7]
        LN_STEPS = 13
        ROUTE_STEPS = 32

        def ffn_pool(pool):
            pool.wait_ge(x_added, NB)

            def rstd_of(c):
                pool.wait_ge(ln_step, c * LN_STEPS + 9)
                pool.tensor_tensor(rstd2[:], var_eps2[:], half_pow[:], ALU.pow).then_inc(pow2_done, 1)

            def input_low(c, par):
                pool.wait_ge(hT_hi_done, c + 1)
                pool.tensor_tensor(hT_lo[:, par], hT[:], hT_hi[:, par].bitcast(F32), ALU.subtract).then_inc(hT_lo_done, 1)

            def hidden_low(T, t):
                pool.wait_ge(hid_hi_done, T + 1)
                if not below(T, 3):
                    pool.wait_ge(down_done, T - 2)
                pool.tensor_tensor(hid_lo[:, t % 3], hid[:, t % 3], hid_hi[:, t % 3].bitcast(F32),
                                   ALU.subtract).then_inc(hid_lo_done, 1)

            rstd_of(0)
            input_low(0, 0)

            def chunk(c, par):
                for t in range(FT):
                    if not (isinstance(c, int) and c == NCH - 1):
                        if t == 2:
                            rstd_of(c + 1)
                        if t == 7:
                            input_low(c + 1, 1 - par)
                    hidden_low(c * FT + t, t)

            each_chunk(pool, chunk)

        def ffn_tensor(pe):
            pe.wait_ge(x_added, NB)
            pe.wait_ge(raw_lo, RAW_LOTS * PIECES)

            def input_transposes(c):
                pe.wait_ge(ln_step, c * LN_STEPS + LN_STEPS)
                for k in range(TPC):
                    ins = pe.transpose(pX[:, k * P:(k + 1) * P], xhat2[:, k, :], ident[:])
                ins.then_inc(xT_ps, 1)

            def logits(c, par):
                pe.wait_ge(hT_lo_done, c + 1)
                for k in range(TPC):
                    toks = slice(k * P, (k + 1) * P)
                    ins = three(pe, pX[:, k * E:(k + 1) * E], hT_hi[:, par, toks], hT_lo[:, par, toks], gwT_hi[:], gwT_lo[:])
                ins.then_inc(logit_ps, 1)

            def weight_transposes(c):
                pe.wait_ge(route_step, c * ROUTE_STEPS + ROUTE_STEPS)
                for k in range(TPC):
                    ins = pe.transpose(pX[0:2 * RW, k * P:(k + 1) * P], cw_parts[:, k, :].bitcast(F32), ident[:])
                ins.then_inc(cwT_ps, 1)

            def gate_up(T, t, par, q):
                for w, (dst, free, done) in enumerate(((pG[q], silu_done, g_ps), (pU[q], au_done, u_ps))):
                    if not below(T, 2):
                        pe.wait_ge(free, T - 1)
                    three(pe, dst[:], wgu_hi[:, w, t, :], wgu_lo[:, w, t, :], hT_hi[:, par], hT_lo[:, par]).then_inc(done, 1)

            def weights_out(T, t, par, c):
                if t >= 2:
                    pe.wait_ge(hid_done, T - 1)
                elif not below(T, FT):
                    pe.wait_ge(hid_done, T - 2)
                if t == 0:
                    pe.wait_ge(cwT_done, c + 1)
                pe.matmul(pC[t % 2][:], pick[0:2 * RW, t, :], cwT[:, par, :], start=True, stop=True).then_inc(c_ps, 1)

            def down(T, t, c):
                pe.wait_ge(hid_lo_done, T + 1)
                if t == 0 and not (isinstance(c, int) and c == 0):
                    pe.wait_ge(yT_done, c)
                K = P if t < WT else EI
                three(pe, pY[:], wd_hi[0:K, t, :], wd_lo[0:K, t, :], hid_hi[0:K, t % 3], hid_lo[0:K, t % 3],
                      start=(t == 0), stop=(t == FT - 1)).then_inc(down_done, 1)

            def result_transposes(c):
                pe.wait_ge(yT_done, c + 1)
                if not (isinstance(c, int) and c == NCH - 1):
                    pe.wait_ge(cwT_done, c + 2)
                for k in range(TPC):
                    ins = pe.transpose(pX[:, k * P:(k + 1) * P], yT[:, k * P:(k + 1) * P], ident[:])
                ins.then_inc(yT_ps, 1)

            input_transposes(0)
            logits(0, 0)
            weight_transposes(0)

            def chunk(c, par):
                first, last = isinstance(c, int) and c == 0, isinstance(c, int) and c == NCH - 1
                for t in range(FT):
                    T = c * FT + t
                    gate_up(T, t, par, (FT * par + t) % 2)
                    if t < WT:
                        weights_out(T, t, par, c)
                    if t >= 3:
                        down(T - 3, t - 3, c)
                    elif not first:
                        down(T - 3, t - 3 + FT, c - 1)
                    if t == 4 and not first:
                        result_transposes(c - 1)
                    if not last:
                        if t == 6:
                            if not first:
                                pe.wait_ge(y_done, c)
                            input_transposes(c + 1)
                        if t == 9:
                            logits(c + 1, 1 - par)
                        if t == 19:
                            weight_transposes(c + 1)

            each_chunk(pe, chunk)
            for t in (FT - 3, FT - 2, FT - 1):
                down((NCH - 1) * FT + t, t, NCH - 1)
            pe.wait_ge(y_done, NCH - 1)
            result_transposes(NCH - 1)

        def ffn_scalar(act):
            act.wait_ge(x_added, NB)

            def input_high(c, par):
                act.wait_ge(hT_done, c * 2 + 2)
                act.activation(hT_hi[:, par], hT[:], ACT.Copy).then_inc(hT_hi_done, 1)

            def scores_out(c):
                act.wait_ge(logit_ps, c + 1)
                act.activation(sig[:], pX[:, 0:TPC * E].rearrange("p (k e) -> p k e", k=TPC), ACT.Sigmoid).then_inc(sig_done, 1)

            def weights_in(c, par):
                act.wait_ge(cwT_ps, c + 1)
                act.activation(cwT[:, par, :], pX[0:2 * RW, :], ACT.Copy).then_inc(cwT_done, 1)

            def gate_silu(T, q):
                act.wait_ge(g_ps, T + 1)
                if not below(T, 2):
                    act.wait_ge(au_done, T - 1)
                act.activation(act_sb[:, q], pG[q][:], ACT.Silu).then_inc(silu_done, 1)

            def hidden_high(T, t):
                act.wait_ge(hid_done, T + 1)
                if not below(T, 3):
                    act.wait_ge(down_done, T - 2)
                act.activation(hid_hi[:, t % 3], hid[:, t % 3], ACT.Copy).then_inc(hid_hi_done, 1)

            def result_out(c):
                act.wait_ge(down_done, c * FT + FT)
                for s in range(SPC):
                    toks = slice(s * S, (s + 1) * S)
                    ins = act.activation(yT[:, toks], pY[:, toks], ACT.Copy, scale=gbT[:, bass.ds(c * SPC + s, 1)])
                ins.then_inc(yT_done, 1)

            input_high(0, 0)
            scores_out(0)
            weights_in(0, 0)

            def chunk(c, par):
                first, last = isinstance(c, int) and c == 0, isinstance(c, int) and c == NCH - 1
                for t in range(FT):
                    T = c * FT + t
                    if t == 3 and not first:
                        result_out(c - 1)
                    gate_silu(T, (FT * par + t) % 2)
                    if t == 20 and not last:
                        weights_in(c + 1, 1 - par)
                    if t:
                        hidden_high(T - 1, t - 1)
                    elif not first:
                        hidden_high(T - 1, FT - 1)
                    if not last:
                        if t == 7:
                            input_high(c + 1, 1 - par)
                        if t == 10:
                            scores_out(c + 1)

            each_chunk(act, chunk)
            hidden_high(NCH * FT - 1, FT - 1)
            result_out(NCH - 1)

        def ffn_vector(dve):
            def layer_norm(c, part):
                def xt(k):
                    return x_all[:, bass.ds(c * TPC + k, 1), :].rearrange("p a d -> p (a d)")

                base = c * LN_STEPS
                if part < 2:
                    for k in range(part * 2, part * 2 + 2):
                        dve.bn_stats(bnst2[:, k, :], xt(k)).then_inc(ln_step, 1)
                if part == 1:
                    wait_apart(dve, ln_step, base + 4, 5)
                    for k in range(TPC):
                        dve.bn_aggr(mv2[:, k, :], bnst2[:, k, :]).then_inc(ln_step, 1)
                    dve.wait_ge(ln_step, base + 8)
                    dve.tensor_scalar(var_eps2[:], mv2[:, :, 1], LN_EPS, None, ALU.add).then_inc(ln_step, 1)
                if part >= 2:
                    dve.wait_ge(pow2_done, c + 1)
                    for k in range(part * 2 - 4, part * 2 - 2):
                        dve.tensor_scalar(xhat2[:, k, :], xt(k), mv2[:, k, 0:1], rstd2[:, k:k + 1],
                                          ALU.subtract, ALU.mult).then_inc(ln_step, 1)

            def input_out(c):
                dve.wait_ge(xT_ps, c + 1)
                for s in range(SPC):
                    toks = slice(s * S, (s + 1) * S)
                    dve.tensor_scalar(hT[:, toks], pX[:, toks], modT[:, 4, bass.ds(c * SPC + s, 1)],
                                      modT[:, 3, bass.ds(c * SPC + s, 1)], ALU.mult, ALU.add).then_inc(hT_done, 1)

            def route(c, part):
                base = c * ROUTE_STEPS
                G8 = E // N_GROUP
                grouped = sel[:].rearrange("p k (g e) -> p (k g) e", e=G8)
                m1, m2, cnt, t1, t2, rank = [gtop[:, i].rearrange("p k g -> p (k g)") for i in range(6)]
                four = [P, TPC, N_GROUP, N_GROUP]
                theirs = gtop[:, 0].rearrange("p k (a i) -> p k a i", a=1).broadcast_to(four)
                own = gtop[:, 0].rearrange("p k (j a) -> p k j a", a=1).broadcast_to(four)
                early = earlier[:].rearrange("p (a j) i -> p a j i", a=1).broadcast_to(four)
                bias = bias_row[:].rearrange("p (a e) -> p a e", a=1).broadcast_to([P, TPC, E])
                scale = wsum[:, 1].rearrange("p (k a) -> p k a", a=1).broadcast_to([P, TPC, E])
                experts = iota_e[:].rearrange("p (a e) -> p a e", a=1).broadcast_to([P, TOP_K, E])

                def over_e(v):
                    return v.rearrange("p (a b) -> p a b", b=1).broadcast_to([P, TPC * N_GROUP, G8])

                def largest(k):
                    return dve.max(top8[:, k, :], masked[:, k, :])

                def places(k):
                    return dve.max_index(idx8[:, k, :], top8[:, k, :], masked[:, k, :])

                def marks(k):
                    place = idxf[:, k].rearrange("p (i a) -> p i a", a=1).broadcast_to([P, TOP_K, E])
                    return dve.tensor_tensor(chosen[:, k], experts, place, ALU.is_equal)

                def mark_sum(k):
                    return dve.tensor_reduce(masked[:, k], chosen[:, k].rearrange("p i e -> p e i"), AX_X, ALU.add)

                def per_tile(f):
                    return [f(k) for k in range(TPC)][-1]

                steps = [
                    lambda: dve.tensor_tensor(sel[:], sig[:], bias, ALU.add),
                    lambda: dve.tensor_reduce(m1, grouped, AX_X, ALU.max),
                    lambda: dve.tensor_tensor(dup[:], grouped, over_e(m1), ALU.is_equal),
                    lambda: dve.tensor_reduce(cnt, dup[:], AX_X, ALU.add),
                    lambda: dve.scalar_tensor_tensor(out=dup[:], in0=dup[:], scalar=-BIG, in1=grouped, op0=ALU.mult, op1=ALU.add),
                    lambda: dve.tensor_reduce(m2, dup[:], AX_X, ALU.max),
                    lambda: dve.tensor_scalar(t1, cnt, 1.5, BIG, ALU.is_ge, ALU.mult),
                    lambda: dve.scalar_tensor_tensor(out=t2, in0=t1, scalar=-BIG, in1=m1, op0=ALU.add, op1=ALU.add),
                    lambda: dve.tensor_tensor(m2, m2, t2, ALU.max),
                    lambda: dve.tensor_tensor(m1, m1, m2, ALU.add),
                    lambda: dve.tensor_tensor(ge4[:], theirs, own, ALU.is_ge),
                    lambda: dve.tensor_tensor(gt4[:], theirs, own, ALU.is_gt),
                    lambda: dve.tensor_tensor(ge4[:], ge4[:], early, ALU.mult),
                    lambda: dve.tensor_tensor(gt4[:], gt4[:], ge4[:], ALU.max),
                    lambda: dve.tensor_reduce(rank, gt4[:].rearrange("p k j i -> p (k j) i"), AX_X, ALU.add),
                    lambda: dve.tensor_scalar(t1, rank, 1.5, -BIG, ALU.is_ge, ALU.mult),
                    lambda: dve.tensor_tensor(masked[:].rearrange("p k (g e) -> p (k g) e", e=G8), grouped, over_e(t1), ALU.add),
                    lambda: per_tile(largest),
                    lambda: per_tile(places),
                    lambda: dve.tensor_copy(idxf[:], idx8[:, :, 0:TOP_K]),
                    lambda: per_tile(marks),
                    lambda: per_tile(mark_sum),
                    lambda: dve.tensor_tensor(masked[:], masked[:], sig[:], ALU.mult),
                    lambda: dve.tensor_reduce(wsum[:, 0], masked[:], AX_X, ALU.add),
                    lambda: dve.tensor_scalar(wsum[:, 1], wsum[:, 0], 1e-20, None, ALU.add),
                    lambda: dve.reciprocal(wsum[:, 0], wsum[:, 1]),
                    lambda: dve.tensor_scalar(wsum[:, 1], wsum[:, 0], ROUTED_SCALE, None, ALU.mult),
                    lambda: dve.tensor_tensor(cw[:, :, 0:E], masked[:], scale, ALU.mult),
                    lambda: dve.tensor_tensor(cw[:, :, E:RW], chosen[:, :, 0, 0:E:2], chosen[:, :, 0, 1:E:2], ALU.add),
                    lambda: dve.tensor_scalar(cw[:, :, E:RW], cw[:, :, E:RW], ANCHOR_ALPHA, None, ALU.mult),
                    lambda: dve.tensor_copy(cw_parts[:, :, 0:RW], cw[:]),
                    lambda: dve.tensor_tensor(cw_parts[:, :, RW:2 * RW], cw[:], cw_parts[:, :, 0:RW].bitcast(F32), ALU.subtract),
                ]
                assert len(steps) == ROUTE_STEPS
                if part == 0:
                    dve.wait_ge(sig_done, c + 1)
                for n in range(ROUTE_AT[part], ROUTE_AT[part + 1]):
                    if n in (LARGEST, LARGEST + 1):
                        wait_apart(dve, route_step, base + n, 6 + n - LARGEST)
                    elif n:
                        dve.wait_ge(route_step, base + n)
                    steps[n]().then_inc(route_step, 1)

            def hidden(T, t, q):
                dve.wait_ge(silu_done, T + 1)
                dve.wait_ge(u_ps, T + 1)
                dve.tensor_tensor(prod_sb[:, q], pU[q][:], act_sb[:, q], ALU.mult).then_inc(au_done, 1)

            def weigh(T, t, q, c):
                dve.wait_ge(au_done, T + 1)
                if not below(T, 3):
                    dve.wait_ge(hid_lo_done, T - 2)
                if t == WT:
                    dve.tensor_copy(hid[:, t % 3], prod_sb[:, q]).then_inc(hid_done, 1)
                    return
                dve.wait_ge(c_ps, c * WT + (t + 1))
                dve.tensor_tensor(hid[:, t % 3], pC[t % 2][:], prod_sb[:, q], ALU.mult).then_inc(hid_done, 1)

            def residual_out(c):
                dve.wait_ge(yT_ps, c + 1)
                t = x_all[:, bass.ds(c * TPC, TPC), :]
                dve.tensor_tensor(t, pX[:].rearrange("p (k d) -> p k d", k=TPC), t, ALU.add).then_inc(y_done, 1)

            dve.wait_ge(x_added, NB)
            for part in range(4):
                layer_norm(0, part)
            input_out(0)
            for part in range(ROUTE_PARTS):
                route(0, part)

            def chunk(c, par):
                first, last = isinstance(c, int) and c == 0, isinstance(c, int) and c == NCH - 1
                for t in range(FT):
                    q = (FT * par + t) % 2
                    T = c * FT + t
                    hidden(T, t, q)
                    if t == 5 and not first:
                        residual_out(c - 1)
                    if not last:
                        if t in (0, 1, 4, 5):
                            layer_norm(c + 1, (0, 1, 2, 2, 2, 3)[t])
                        if t == 7:
                            input_out(c + 1)
                        if 10 <= t < 10 + ROUTE_PARTS:
                            route(c + 1, t - 10)
                    weigh(T, t, q, c)

            each_chunk(dve, chunk)
            residual_out(NCH - 1)

        ROUTE_AT = [0, 5, 10, 16, 18, 20, 22, 28, 32]
        ROUTE_PARTS = len(ROUTE_AT) - 1
        LARGEST = 17

        def prologue_dve(dve):
            steps, seen = [0], [0]

            def then(ins):
                steps[0] += 1
                ins.then_inc(pro_step, 1)
                dve.wait_ge(pro_step, steps[0])

            def bank():
                seen[0] += 1
                dve.wait_ge(pro_pe, seen[0])
                return banks[(seen[0] - 1) % 8]

            dve.tensor_copy(scT, bank()[:, 0:NB]).then_inc(pro_ev, 1)
            t = bank()
            then(dve.tensor_copy(gwT_hi[:], t[:, 0:E]))
            dve.tensor_tensor(gwT_lo[:], t[:, 0:E], gwT_hi[:].bitcast(F32), ALU.subtract).then_inc(pro_ev, 1)
            t = bank()
            dve.tensor_scalar(mod_rows[:, 0:D], t[0:NB, D:2 * D], 1.0, None, ALU.add).then_inc(mod_rows_made, 1)
            dve.tensor_copy(mod_rows[:, D:2 * D], t[0:NB, 0:D]).then_inc(mod_rows_made, 1)
            dve.wait_ge(mod_rows_made, 2)
            dve.engine_nop().then_inc(pro_ev, 1)
            t = bank()
            then(dve.tensor_copy(modT[:], t[:, 0:6 * NB].rearrange("p (m b) -> p m b", m=6)))
            dve.engine_nop().then_inc(pro_ev, 1)
            then(dve.tensor_scalar(modT[:, 4], modT[:, 4], 1.0, None, ALU.add))
            for m, dst in ((2, gaT), (5, gbT)):
                g = modT[:, m]
                then(dve.scalar_tensor_tensor(out=mod_tmp[:, 0], in0=g, scalar=-1.0, in1=g, op0=ALU.mult, op1=ALU.max))
                then(dve.tensor_scalar(mod_tmp[:, 0], mod_tmp[:, 0], 0.25, None, ALU.max))
                then(dve.tensor_scalar(mod_tmp[:, 1], g, 0.0, 2.0, ALU.is_ge, ALU.mult))
                then(dve.scalar_tensor_tensor(out=dst[:], in0=mod_tmp[:, 1], scalar=-1.0, in1=mod_tmp[:, 0], op0=ALU.add, op1=ALU.mult))
            for jj in range(0, PAIRS, 4):
                for ch in range(3):
                    t = bank()
                    if ch < 2:
                        hi = wqk_hi[:, ch, jj:jj + 4, :].rearrange("p j n -> p (j n)")
                        lo = wqk_lo[:, ch, jj:jj + 4, :].rearrange("p j n -> p (j n)")
                    else:
                        hi, lo = wv_hi[:, jj * P:(jj + 4) * P], wv_lo[:, jj * P:(jj + 4) * P]
                    sign = -1.0 if ch == 0 else 1.0
                    then(dve.tensor_scalar(hi, t[:], sign, None, ALU.mult))
                    dve.scalar_tensor_tensor(out=lo, in0=t[:], scalar=sign, in1=hi.bitcast(F32), op0=ALU.mult,
                                             op1=ALU.subtract).then_inc(pro_ev, 1)
            for jj in range(0, PAIRS, 4):
                t = bank()
                hi = woT_hi[:, jj:jj + 4, :].rearrange("p j n -> p (j n)")
                then(dve.tensor_copy(hi, t[:]))
                dve.tensor_tensor(woT_lo[:, jj:jj + 4, :].rearrange("p j n -> p (j n)"), t[:], hi.bitcast(F32),
                                  ALU.subtract).then_inc(pro_ev, 1)
            dve.wait_ge(bias_loaded, 48)
            dve.tensor_scalar(nbq[:], bqkv[:, :, 0], -1.0, None, ALU.mult).then_inc(nbq_made, 1)
            for j in range(PAIRS + 1):
                if j < PAIRS:
                    dve.tensor_scalar(bv_diag[:, j % 2, :], ident[:], bqkv[:, j, 2:3], None, ALU.mult).then_inc(bv_diag_made, 1)
                if j:
                    dve.tensor_copy(bv_rows[:, (j - 1) * P:j * P], bank()[:, 0:P]).then_inc(pro_ev, 1)
            dve.wait_ge(pro_ev, 20)
            dve.wait_ge(nbq_made, 1)

        @block.sync
        def _(sp):
            sp.dma_start(c_sb, cond).then_inc(mod_loaded, 16)
            sp.dma_start(wmod_sb, wmod).then_inc(mod_loaded, 16)
            sp.dma_start(gw_rows, gate_w).then_inc(mod_loaded, 16)
            sp.dma_start(x_all[:, 0:2 * KT, :], x[0:2].rearrange("b (k p) d -> p (b k) d", p=P)).then_inc(x_first, 16)
            sp.dma_start(wq_rows, W_qkv.rearrange("(j n c) i -> n j c i", n=P, c=3)).then_inc(w_loaded, 16)
            sp.dma_start(wo_rows, W_o).then_inc(w_loaded, 16)
            sp.dma_start(bqkv[:], b_qkv.rearrange("(j n c) -> n j c", n=P, c=3)).then_inc(bias_loaded, 16)
            sp.dma_start(bo_col[:], b_o.rearrange("(n a) -> n a", a=1)).then_inc(bias_loaded, 16)
            sp.dma_start(bias_row[:], gate_bias.rearrange("(a n) -> a n", a=1).broadcast_to([P, E])).then_inc(bias_loaded, 16)
            for b0 in range(2, NB, 10):
                sp.dma_start(x_all[:, b0 * KT:(b0 + 10) * KT, :],
                             x[b0:b0 + 10].rearrange("b (k p) d -> p (b k) d", p=P)).then_inc(x_loaded, 16)
            sp.wait_ge(mod_rows_made, 2)
            sp.dma_start(mod_dram, mod_rows).then_inc(mod_stored, 16)
            sp.wait_ge(mod_stored, 16)

            def mod_rows_load(b, par):
                sp.dma_start(mod_bc[:, par, :], mod_dram[bass.ds(b, 1), :].broadcast_to([P, 2 * D])).then_inc(mod_rows_in[par], 16)

            mod_rows_load(0, 0)
            mod_rows_load(1, 1)
            sp.wait_ge(pro_ev, 4)
            sp.wait_ge(consts_made, 7)
            for n in range(RAW_LOTS):
                if n:
                    sp.wait_ge(raw_lo, n * PIECES)
                for dst, src in raw_lot(n):
                    sp.dma_start(dst, src).then_inc(raw_loaded, 16)

            with sp.Fori(1, NB // 2) as i:
                for k in range(2):
                    sp.wait_ge(hmod_step, i * 4 + (2 * k - 2))
                    mod_rows_load(i * 2 + k, k)

            out_v = out.rearrange("b (k p) d -> p (b k) d", p=P)
            with sp.Fori(0, NCH) as c:
                sp.wait_ge(y_done, c + 1)
                sp.dma_start(out_v[:, bass.ds(c * TPC, TPC), :], x_all[:, bass.ds(c * TPC, TPC), :]).then_inc(y_stored, 16)
            sp.wait_ge(y_stored, 16 * NCH)

        @block.gpsimd
        def _(pool):
            pool.memset(ones[:], 1.0).then_inc(consts_made, 1)
            pool.memset(ident[:], 0.0).then_inc(pick_made, 1)
            pool.memset(causal[:], 0.0).then_inc(pick_made, 1)
            pool.memset(half_pow[:], -0.5).then_inc(consts_made, 1)
            pool.memset(earlier[:], 1.0).then_inc(pick_made, 1)
            pool.wait_ge(pick_made, 3)
            pool.affine_select(out=ident[:], in_=ident[:], compare_op=ALU.not_equal, fill=1.0, base=0,
                               pattern=[[-1, P]], channel_multiplier=1).then_inc(consts_made, 1)
            pool.affine_select(out=causal[:, 0:S], in_=causal[:, 0:S], compare_op=ALU.is_ge, fill=BIG, base=0,
                               pattern=[[1, S]], channel_multiplier=-1)
            pool.affine_select(out=causal[:, S:SW], in_=causal[:, S:SW], compare_op=ALU.is_ge, fill=BIG, base=0,
                               pattern=[[1, P]], channel_multiplier=-1).then_inc(consts_made, 1)
            pool.affine_select(out=earlier[:], in_=earlier[:], compare_op=ALU.is_ge, fill=0.0, base=-1,
                               pattern=[[1, N_GROUP], [-1, N_GROUP]], channel_multiplier=0).then_inc(consts_made, 1)
            pool.iota(iota_e[:], pattern=[[1, E]], base=0, channel_multiplier=0,
                      allow_small_or_imprecise_dtypes=True).then_inc(consts_made, 1)
            pool.memset(stage[:, WT * P:FT * P], 0.0).then_inc(consts_made, 1)

            def rstd_of(b, par):
                pool.wait_ge(norm_step, b * NORM_STEPS + 5)
                pool.tensor_tensor(rstd[:, 0:KT], var_eps[:, 0:KT], half_pow[:, 0:KT], ALU.pow).then_inc(pow_done, 1)

            def modulate(b, par):
                pool.wait_ge(norm_step, b * NORM_STEPS + 7)
                pool.wait_ge(mod_rows_in[par], b * 8 + (16 - 8 * par))
                m = mod_bc[:, par, :].rearrange("p (a k d) -> p a k d", a=2, k=1)
                pool.tensor_tensor(hmul[:], xhat[:, 0:KT, :], m[:, 0].broadcast_to([P, KT, D]), ALU.mult).then_inc(hmod_step, 1)
                pool.wait_ge(hmod_step, b * 2 + 1)
                pool.tensor_tensor(hmod[:], hmul[:], m[:, 1].broadcast_to([P, KT, D]), ALU.add).then_inc(hmod_step, 1)

            def rrms_of(b, par):
                pool.wait_ge(norm_step, b * NORM_STEPS + 10)
                pool.tensor_tensor(rrms[:], ms_eps[:], half_pow[:, 0:KT], ALU.pow).then_inc(pow_done, 1)

            def scale_v(g, j, par, v_need):
                pool.wait_ge(rz_done, g + 1)
                pool.wait_ge(v_done, v_need)
                if not (isinstance(g, int) and g < 2):
                    pool.wait_ge(z_ps, g - 1)
                pool.tensor_tensor(
                    vn[:, j % 2].rearrange("p k (h d) -> p k h d", d=DH),
                    v_sb[:, par, :, j * P:(j + 1) * P].rearrange("p k (h d) -> p k h d", d=DH),
                    rz[:, j % 2].rearrange("p k (h a) -> p k h a", a=1).broadcast_to([P, KT, 2, DH]),
                    ALU.mult).then_inc(vn_done, 1)

            rstd_of(0, 0)
            modulate(0, 0)
            rrms_of(0, 0)
            pool.memset(pick[:].bitcast(F32), 0.0).then_inc(pick_made, 1)
            pool.wait_ge(pick_made, 4)
            for n, (t0, nt, first, per) in enumerate(((0, ET, 0, P // EI), (ET, AT, E, P // AI))):
                v = pick[:, t0:t0 + nt, :].rearrange("p t (w n) -> p t w n", w=per)
                for part in range(2):
                    pool.affine_select(out=v, in_=v, compare_op=ALU.not_equal, fill=1.0, base=-first - part * RW,
                                       pattern=[[-per, nt], [-1, per], [0, P // per]],
                                       channel_multiplier=1).then_inc(pick_made, 1)
                    pool.wait_ge(pick_made, 5 + 2 * n + part)

            def split_low(n):
                raw, hi, lo = raw_piece(n)
                pool.wait_ge(raw_hi, n + 1)
                pool.tensor_tensor(lo, raw, hi.bitcast(F32), ALU.subtract).then_inc(raw_lo, 1)

            def sequence(b, par):
                for j in range(PAIRS):
                    if j:
                        scale_v(b * PAIRS + (j - 1), j - 1, par, b * 4 + (2 if j <= PAIRS // 2 else 4))
                    elif not is_first(b):
                        scale_v(b * PAIRS - 1, PAIRS - 1, 1 - par, b * 4)
                    if not is_last(b):
                        if j == 0:
                            rstd_of(b + 1, 1 - par)
                        if j == 1:
                            modulate(b + 1, 1 - par)
                        if j == 2:
                            rrms_of(b + 1, 1 - par)
                    for n in raw_pieces(b * PAIRS + j):
                        split_low(n)

            each_sequence(pool, sequence)
            scale_v(NB * PAIRS - 1, PAIRS - 1, 1, NB * 4)

            ffn_pool(pool)

        def three(pe, dst, lhs_hi, lhs_lo, rhs_hi, rhs_lo, start=True, stop=True):
            pe.matmul(dst, lhs_hi, rhs_hi, start=start, stop=False)
            pe.matmul(dst, lhs_hi, rhs_lo, start=False, stop=False)
            return pe.matmul(dst, lhs_lo, rhs_hi, start=False, stop=stop)

        def prologue_pe(pe):
            n = [0]

            def bank():
                if n[0] >= 8:
                    pe.wait_ge(pro_ev, n[0] - 7)
                n[0] += 1
                return banks[(n[0] - 1) % 8]

            pe.wait_ge(consts_made, 7)
            pe.wait_ge(silu_c_done, 1)
            pe.transpose(bank()[:, 0:NB], sc_sb, ident[0:NB, 0:NB]).then_inc(pro_pe, 1)
            pe.wait_ge(mod_loaded, 48)
            pe.transpose(bank()[:, 0:E], gw_rows, ident[0:E, 0:E]).then_inc(pro_pe, 1)
            pe.wait_ge(pro_ev, 1)
            t = bank()
            pe.matmul(t[0:NB, 0:2 * D], scT, wmod_sb[:, 0:2 * D], start=True, stop=True).then_inc(pro_pe, 1)
            t = bank()
            for m in range(6):
                ins = pe.matmul(t[:, m * NB:(m + 1) * NB], wmod_sb[:, m * D:(m + 1) * D], scT, start=True, stop=True)
            ins.then_inc(pro_pe, 1)
            pe.wait_ge(w_loaded, 32)
            for jj in range(0, PAIRS, 4):
                for c in range(3):
                    t = bank()
                    for k in range(4):
                        ins = pe.transpose(t[:, k * P:(k + 1) * P], wq_rows[:, jj + k, c, :], ident[:])
                    ins.then_inc(pro_pe, 1)
            for jj in range(0, PAIRS, 4):
                t = bank()
                for k in range(4):
                    ins = pe.transpose(t[:, k * P:(k + 1) * P], wo_rows[:, (jj + k) * P:(jj + k + 1) * P], ident[:])
                ins.then_inc(pro_pe, 1)
            for j in range(PAIRS):
                pe.wait_ge(bv_diag_made, j + 1)
                pe.matmul(bank()[:, 0:P], ones[:], bv_diag[:, j % 2, :], start=True, stop=True).then_inc(pro_pe, 1)
            pe.wait_ge(pro_ev, n[0])

        def transpose_normed(pe, b):
            pe.wait_ge(norm_step, b * NORM_STEPS + NORM_STEPS)
            for k in range(KT):
                ins = pe.transpose(pM[1][:, k * P:(k + 1) * P], normed[:, k, :], ident[:])
            ins.then_inc(nT_ps, 1)

        def values(pe, b, par, chunk):
            half, k = chunk // 2, chunk % 2
            if chunk == 0:
                pe.wait_ge(nT_hi_done, b + 1)
                pe.wait_ge(nT_lo_done, b + 1)
            if chunk >= 2:
                pe.wait_ge(v_done, b * 4 + (chunk - 1))
            elif chunk == 0 and not is_first(b):
                if not (isinstance(b, int) and b == 1):
                    pe.wait_ge(x_added, b - 1)
                else:
                    pe.wait_ge(v_done, 3)
            toks = slice(k * P, (k + 1) * P)
            cols = slice(half * 512, (half + 1) * 512)
            three(pe, pM[chunk % 2][:], nT_hi[:, par, toks], nT_lo[:, par, toks], wv_hi[:, cols], wv_lo[:, cols]).then_inc(v_ps, 1)

        def project(pe, g, j, par):
            if not (isinstance(g, int) and g < 2):
                pe.wait_ge(qk_lo_done, g - 1)
            for w in range(2):
                ins = three(pe, pQK[j % 2][:, w * S:(w + 1) * S], wqk_hi[:, w, j, :], wqk_lo[:, w, j, :],
                            nT_hi[:, par], nT_lo[:, par])
            ins.then_inc(qk_ps, 1)

        def scores(pe, g, j):
            pe.wait_ge(qk_lo_done, g + 1)
            for h in range(2):
                if not (isinstance(g, int) and g == 0):
                    pe.wait_ge(s_masked, g * 2 + (h - 1))
                r = slice(h * DH, (h + 1) * DH)
                t = pS[h]
                for k in range(KT):
                    keys = slice(k * P, (k + 1) * P)
                    dst = t[:, 0:S] if k == 0 else t[:, S:SW]
                    ins = three(pe, dst, qk_hi[r, j % 2, 1, keys], qk_lo[r, j % 2, 1, keys],
                                qk_hi[r, j % 2, 0, k * P:S], qk_lo[r, j % 2, 0, k * P:S])
                ins.then_inc(s_ps, 1)

        def attend(pe, g, j):
            pe.wait_ge(e_done, g * 2 + 2)
            pe.wait_ge(vn_done, g + 1)
            if not (isinstance(g, int) and g == 0):
                pe.wait_ge(z_lo_done, g)
            for k in range(KT):
                for h in range(2):
                    src = s_sb[:, (2 * j + h) % 4, :]
                    ins = pe.matmul(pZ[h * DH:(h + 1) * DH, k * P:S], vn[:, j % 2, k, h * DH:(h + 1) * DH],
                                    src[:, 0:S] if k == 0 else src[:, S:SW], start=(k == 0), stop=(k == KT - 1))
            ins.then_inc(z_ps, 1)

        def project_out(pe, g, j, b):
            pe.wait_ge(z_lo_done, g + 1)
            if j == 0 and not is_first(b):
                pe.wait_ge(att_done, b)
            three(pe, pO[:, 0:S], woT_hi[:, j, :], woT_lo[:, j, :], zT_hi[:, j % 2], zT_lo[:, j % 2],
                  start=(j == 0), stop=(j == PAIRS - 1)).then_inc(o_ps, 1)

        def transpose_att(pe, b):
            pe.wait_ge(att_done, b + 1)
            pe.wait_ge(v_done, b * 4 + (4 if is_last(b) else 7))
            for k in range(KT):
                ins = pe.transpose(pM[0][:, k * P:(k + 1) * P], attT[:, k * P:(k + 1) * P], ident[:])
            ins.then_inc(attT_ps, 1)

        @block.tensor
        def _(pe):
            prologue_pe(pe)
            transpose_normed(pe, 0)
            for chunk in range(3):
                values(pe, 0, 0, chunk)
            project(pe, 0, 0, 0)
            project(pe, 1, 1, 0)

            def sequence(b, par):
                for j in range(PAIRS):
                    g = b * PAIRS + j
                    scores(pe, g, j)
                    if j == 0:
                        values(pe, b, par, 3)
                    if j == 3 and not is_first(b):
                        transpose_att(pe, b - 1)
                    if j == 4 and not is_last(b):
                        pe.wait_ge(v_done, b * 4 + 4)
                        transpose_normed(pe, b + 1)
                    if j >= 5 and not is_last(b):
                        values(pe, b + 1, 1 - par, j - 5)
                    if j < PAIRS - 2:
                        project(pe, g + 2, j + 2, par)
                    elif not is_last(b):
                        project(pe, g + 2, j + 2 - PAIRS, 1 - par)
                    if j:
                        attend(pe, g - 1, j - 1)
                    elif not is_first(b):
                        attend(pe, g - 1, PAIRS - 1)
                    if j >= 2:
                        project_out(pe, g - 2, j - 2, b)
                    elif not is_first(b):
                        project_out(pe, g - 2, j - 2 + PAIRS, b - 1)

            each_sequence(pe, sequence)
            attend(pe, NB * PAIRS - 1, PAIRS - 1)
            project_out(pe, NB * PAIRS - 2, PAIRS - 2, last_b)
            project_out(pe, NB * PAIRS - 1, PAIRS - 1, last_b)
            transpose_att(pe, last_b)
            ffn_tensor(pe)

        @block.scalar
        def _(act):
            act.wait_ge(mod_loaded, 48)
            act.activation(sc_sb, c_sb, ACT.Silu).then_inc(silu_c_done, 1)

            def normed_hi(b, par):
                act.wait_ge(nT_ps, b + 1)
                act.activation(nT_hi[:, par], pM[1][:, 0:S], ACT.Copy).then_inc(nT_hi_done, 1)

            def qk_high(g, j):
                act.wait_ge(qk_ps, g + 1)
                if not (isinstance(g, int) and g < 2):
                    act.wait_ge(s_ps, g * 2 - 2)
                act.activation(qk_hi[:, j % 2, 0], pQK[j % 2][:, 0:S], ACT.Identity, bias=nbq[:, j:j + 1])
                act.activation(qk_hi[:, j % 2, 1], pQK[j % 2][:, S:2 * S], ACT.Identity,
                               bias=bqkv[:, j, 1:2]).then_inc(qk_hi_done, 1)

            def exponentials(g, j):
                if not (isinstance(g, int) and g < 2):
                    act.wait_ge(rz_done, g - 1)
                for h in range(2):
                    act.wait_ge(s_masked, g * 2 + (h + 1))
                    n = (2 * j + h) % 4
                    for k in range(KT):
                        cols = slice(0, S) if k == 0 else slice(S, SW)
                        ins = act.activation(s_sb[:, n, cols], s_sb[:, n, cols], ACT.Exp, bias=smin[:, n, k:k + 1],
                                             scale=-1.0, accum_out=zsum[:, j % 2, k, h:h + 1])
                    ins.then_inc(e_done, 1)

            def z_high(g, j):
                act.wait_ge(z_ps, g + 1)
                if not (isinstance(g, int) and g < 2):
                    act.wait_ge(o_ps, g - 1)
                act.activation(zT_hi[:, j % 2], pZ[:, 0:S], ACT.Copy).then_inc(z_hi_done, 1)

            def split_high(n):
                raw, hi, _ = raw_piece(n)
                act.wait_ge(raw_loaded, 48 * (n // PIECES + 1))
                act.activation(hi, raw, ACT.Copy).then_inc(raw_hi, 1)

            normed_hi(0, 0)
            act.wait_ge(nbq_made, 1)
            act.wait_ge(bias_loaded, 48)
            qk_high(0, 0)
            qk_high(1, 1)

            def sequence(b, par):
                for j in range(PAIRS):
                    g = b * PAIRS + j
                    if j >= 2 or not is_first(b):
                        z_high(g - 2, j)
                    exponentials(g, j)
                    if j == 4 and not is_last(b):
                        normed_hi(b + 1, 1 - par)
                    if j < PAIRS - 2 or not is_last(b):
                        qk_high(g + 2, (j + 2) % PAIRS)
                    for n in raw_pieces(g):
                        split_high(n)

            each_sequence(act, sequence)
            z_high(NB * PAIRS - 2, PAIRS - 2)
            z_high(NB * PAIRS - 1, PAIRS - 1)
            ffn_scalar(act)

        @block.vector
        def _(dve):
            prologue_dve(dve)

            def norm(b, par, stage_no):
                base = b * NORM_STEPS
                tiles = [b * KT + k for k in range(KT)]

                def xt(k):
                    return x_all[:, bass.ds(tiles[k], 1), :].rearrange("p a d -> p (a d)")

                if stage_no == 0:
                    for k in range(KT):
                        dve.bn_stats(bnst[:, k, :], xt(k)).then_inc(norm_step, 1)
                    wait_apart(dve, norm_step, base + 2, 4)
                    for k in range(KT):
                        dve.bn_aggr(mv[:, k, :], bnst[:, k, :]).then_inc(norm_step, 1)
                    dve.wait_ge(norm_step, base + 4)
                    dve.tensor_scalar(var_eps[:, 0:KT], mv[:, 0:KT, 1], LN_EPS, None, ALU.add).then_inc(norm_step, 1)
                if stage_no == 1:
                    dve.wait_ge(pow_done, b * 2 + 1)
                    for k in range(KT):
                        dve.tensor_scalar(xhat[:, k, :], xt(k), mv[:, k, 0:1], rstd[:, k:k + 1],
                                          ALU.subtract, ALU.mult).then_inc(norm_step, 1)
                if stage_no == 2:
                    dve.wait_ge(hmod_step, b * 2 + 2)
                    for k in range(KT):
                        dve.tensor_tensor_reduce(sq_junk[:, k, :], hmod[:, k, :], hmod[:, k, :], 1.0, 0.0, ALU.mult,
                                                 ALU.add, sumsq[:, k:k + 1]).then_inc(norm_step, 1)
                    dve.wait_ge(norm_step, base + 9)
                    dve.tensor_scalar(ms_eps[:], sumsq[:], 1.0 / D, RMS_EPS, ALU.mult, ALU.add).then_inc(norm_step, 1)
                if stage_no == 3:
                    dve.wait_ge(pow_done, b * 2 + 2)
                    for k in range(KT):
                        dve.tensor_scalar(normed[:, k, :], hmod[:, k, :], rrms[:, k:k + 1], None,
                                          ALU.mult).then_inc(norm_step, 1)

            def normed_lo(b, par):
                dve.wait_ge(nT_hi_done, b + 1)
                dve.tensor_tensor(nT_lo[:, par], pM[1][:, 0:S], nT_hi[:, par].bitcast(F32), ALU.subtract).then_inc(nT_lo_done, 1)

            def value_rows(b, par, chunk):
                half, k = chunk // 2, chunk % 2
                dve.wait_ge(v_ps, b * 4 + (chunk + 1))
                cols = slice(half * 512, (half + 1) * 512)
                dve.tensor_tensor(v_sb[:, par, k, cols], pM[chunk % 2][:], bv_rows[:, cols], ALU.add).then_inc(v_done, 1)

            def qk_low(g, j):
                dve.wait_ge(qk_hi_done, g + 1)
                bias = (nbq[:, j:j + 1], bqkv[:, j, 1:2])
                for w in range(2):
                    ins = dve.scalar_tensor_tensor(out=qk_lo[:, j % 2, w], in0=pQK[j % 2][:, w * S:(w + 1) * S],
                                                   scalar=bias[w], in1=qk_hi[:, j % 2, w].bitcast(F32),
                                                   op0=ALU.add, op1=ALU.subtract)
                ins.then_inc(qk_lo_done, 1)

            def z_low(g, j):
                dve.wait_ge(z_hi_done, g + 1)
                dve.tensor_tensor(zT_lo[:, j % 2], pZ[:, 0:S], zT_hi[:, j % 2].bitcast(F32),
                                  ALU.subtract).then_inc(z_lo_done, 1)

            def sums(g, j):
                dve.wait_ge(e_done, g * 2 + 2)
                dve.reciprocal(rz[:, j % 2], zsum[:, j % 2]).then_inc(rz_done, 1)

            def mask_and_min(g, j):
                for h in range(2):
                    n = (2 * j + h) % 4
                    if not (isinstance(g, int) and g < 2):
                        dve.wait_ge(z_ps, g - 1)
                    wait_apart(dve, s_ps, g * 2 + (h + 1), n)
                    for k in range(KT):
                        cols = slice(0, S) if k == 0 else slice(S, SW)
                        ins = dve.tensor_tensor_reduce(s_sb[:, n, cols], pS[h][:, cols], causal[:, cols], 1.0, 3e38,
                                                       ALU.add, ALU.min, smin[:, n, k:k + 1])
                    ins.then_inc(s_masked, 1)

            def att_out(b):
                dve.wait_ge(o_ps, b * PAIRS + PAIRS)
                dve.tensor_scalar(attT[:], pO[:, 0:S], bo_col[:, 0:1], gaT[:, bass.ds(b, 1)], ALU.add, ALU.mult).then_inc(att_done, 1)

            def residual(b):
                dve.wait_ge(attT_ps, b + 1)
                t = x_all[:, bass.ds(b * KT, KT), :]
                dve.tensor_tensor(t, pM[0][:, 0:S].rearrange("p (k d) -> p k d", k=KT), t, ALU.add).then_inc(x_added, 1)

            dve.wait_ge(x_first, 16)
            for st in range(4):
                norm(0, 0, st)
            normed_lo(0, 0)
            for chunk in range(3):
                value_rows(0, 0, chunk)
            qk_low(0, 0)
            dve.wait_ge(x_loaded, 48)

            def sequence(b, par):
                for j in range(PAIRS):
                    g = b * PAIRS + j
                    if j:
                        sums(g - 1, j - 1)
                    elif not is_first(b):
                        sums(g - 1, PAIRS - 1)
                    if j >= 2 or not is_first(b):
                        z_low(g - 2, j)
                    if j == 2 and not is_first(b):
                        att_out(b - 1)
                    mask_and_min(g, j)
                    if not (is_last(b) and j == PAIRS - 1):
                        qk_low(g + 1, (j + 1) % PAIRS)
                    if j == 0:
                        value_rows(b, par, 3)
                    if j == 3 and not is_first(b):
                        residual(b - 1)
                    if j == 4 and not is_last(b):
                        normed_lo(b + 1, 1 - par)
                    if j >= 5 and not is_last(b):
                        value_rows(b + 1, 1 - par, j - 5)
                    if j < 4 and not is_last(b):
                        norm(b + 1, 1 - par, j)

            each_sequence(dve, sequence)
            sums(NB * PAIRS - 1, PAIRS - 1)
            z_low(NB * PAIRS - 2, PAIRS - 2)
            z_low(NB * PAIRS - 1, PAIRS - 1)
            att_out(last_b)
            residual(last_b)
            ffn_vector(dve)



_INS = ['L0_attn_x', 'L0_attn_W_qkv', 'L0_attn_b_qkv', 'L0_attn_W_o', 'L0_attn_b_o', 'L0_ffn_gate_weight',
        'L0_ffn_gate_bias', 'L0_ffn_w_gate', 'L0_ffn_w_up', 'L0_ffn_w_down', 'L0_ffn_shared_w_gate',
        'L0_ffn_shared_w_up', 'L0_ffn_shared_w_down', 'L0_ffn_anchor_w_gate', 'L0_ffn_anchor_w_up',
        'L0_ffn_anchor_w_down', 'L0_c', 'L0_wmod']


def kernel(**inputs):
    import numpy as _np
    import concourse.bacc as _bacc
    from concourse import mybir as _mybir
    from concourse.bass_utils import run_bass_kernel_spmd as _run

    nc = _bacc.Bacc("TRN2", target_bir_lowering=False, num_devices=1)
    arrays, args = {}, []
    for name in _INS:
        a = _np.ascontiguousarray(inputs[name])
        arrays[f"in_{name}_dram"] = a
        args.append(nc.dram_tensor(f"in_{name}_dram", a.shape, _mybir.dt.from_np(a.dtype), kind="ExternalInput").ap())
    shape = inputs['L0_attn_x'].shape
    args.append(nc.dram_tensor("out_0_dram", shape, _mybir.dt.float32, kind="ExternalOutput").ap())
    adaln_block_kernel(nc, *args)
    r = _run(nc, [arrays], core_ids=[0])
    return r.results[0]["out_0_dram"]
```

```python
from contextlib import ExitStack

import concourse.bass as bass
from concourse import mybir

ALU = mybir.AluOpType
ACT = mybir.ActivationFunctionType
F32 = mybir.dt.float32
F32R = mybir.dt.float32r
U32 = mybir.dt.uint32
AX_X = mybir.AxisListType.X

P = 128
LN_EPS = 1e-05
RMS_EPS = 1.1920929e-07
ROUTED_SCALE = 0.2
ANCHOR_ALPHA = 0.1
TOP_K = 6
N_GROUP = 4
BIG = 1e30


def adaln_block_kernel(nc, x, W_qkv, b_qkv, W_o, b_o, gate_w, gate_bias, w_gate, w_up, w_down,
                       sh_gate, sh_up, sh_down, an_gate, an_up, an_down, cond, wmod, out):
    NB, S, D = x.shape
    KT = S // P
    HD = W_o.shape[1]
    DH = 64
    PAIRS = HD // P
    E, _, EI = w_gate.shape
    L, _, AI = an_gate.shape
    ET = E * EI // P
    AT = L * AI // P
    WT = ET + AT
    FT = WT + 1
    SW = S + P
    CH = 512
    NCH = NB * S // CH
    TPC = CH // P
    SPC = CH // S
    RW = E + L
    NORM_STEPS = 10

    mod_dram = nc.dram_tensor("mod_rows", (NB, 2 * D), F32, kind="Internal").ap()

    with ExitStack() as ctx:
        memory = ctx

        def sb(name, shape, dt=F32):
            return memory.enter_context(nc.sbuf_tensor(name, shape, dt))

        def pb(name):
            return ctx.enter_context(nc.psum_tensor(name, [P, 512], F32))

        def sem(name):
            return ctx.enter_context(nc.semaphore(name))

        ident = sb("ident", [P, P])
        ones = sb("ones", [P, P])
        causal = sb("causal", [P, SW])
        earlier = sb("earlier", [P, N_GROUP, N_GROUP])
        iota_e = sb("iota_e", [P, E])
        unused = sb("unused", [P, 8])
        half_pow = sb("half_pow", [P, TPC])
        pick = sb("pick", [P, WT, P], F32R)
        wqk_hi = sb("wqk_hi", [P, 2, PAIRS, P], F32R)
        wqk_lo = sb("wqk_lo", [P, 2, PAIRS, P], F32R)
        wv_hi = sb("wv_hi", [P, HD], F32R)
        wv_lo = sb("wv_lo", [P, HD], F32R)
        woT_hi = sb("woT_hi", [P, PAIRS, D], F32R)
        woT_lo = sb("woT_lo", [P, PAIRS, D], F32R)
        bqkv = sb("bqkv", [P, PAIRS, 3])
        nbq = sb("nbq", [P, PAIRS])
        bv_rows = sb("bv_rows", [P, HD])
        bo_col = sb("bo_col", [P, 1])
        bias_row = sb("bias_row", [P, E])
        wgu_hi = sb("wgu_hi", [P, 2, FT, P], F32R)
        wgu_lo = sb("wgu_lo", [P, 2, FT, P], F32R)
        wd_hi = sb("wd_hi", [P, FT, D], F32R)
        wd_lo = sb("wd_lo", [P, FT, D], F32R)
        gwT_hi = sb("gwT_hi", [P, E], F32R)
        gwT_lo = sb("gwT_lo", [P, E], F32R)
        modT = sb("modT", [P, 6, NB])
        mod_tmp = sb("mod_tmp", [P, 2, NB])
        gaT = sb("gaT", [P, NB])
        bogaT = sb("bogaT", [P, NB])
        gbT = sb("gbT", [P, NB])
        x_all = sb("x_all", [P, NB * KT, D])

        memory = ExitStack()
        stage = sb("stage", [P, 2, FT * P])
        memory.close()
        memory = ctx

        mv2 = sb("mv2", [P, TPC, 2])
        bnst2 = sb("bnst2", [P, TPC, 6])
        var_eps2 = sb("var_eps2", [P, TPC])
        rstd2 = sb("rstd2", [P, TPC])
        xhat2 = sb("xhat2", [P, TPC, D])
        hT_hi = sb("hT_hi", [P, 2, CH], F32R)
        hT_lo = sb("hT_lo", [P, 2, CH], F32R)
        sig = sb("sig", [P, TPC, E])
        sel = sb("sel", [P, TPC, E])
        dup = sb("dup", [P, TPC * N_GROUP, E // N_GROUP])
        masked = sb("masked", [P, TPC, E])
        gtop = sb("gtop", [P, 6, TPC, N_GROUP])
        ge4 = sb("ge4", [P, TPC, N_GROUP, N_GROUP])
        gt4 = sb("gt4", [P, TPC, N_GROUP, N_GROUP])
        top8 = sb("top8", [P, TPC, 8])
        idx8 = sb("idx8", [P, TPC, 8], U32)
        idxf = sb("idxf", [P, TPC, TOP_K])
        chosen = sb("chosen", [P, TPC, TOP_K, E])
        hT = chosen[:].rearrange("p k i e -> p (k i e)")[:, 0:CH]
        cw = sb("cw", [P, TPC, RW])
        wsum = sb("wsum", [P, 2, TPC])
        cw_parts = sb("cw_parts", [P, TPC, 2 * RW], F32R)
        cwT = sb("cwT", [2 * RW, 2, CH], F32R)

        memory = ExitStack()
        bnst = sb("bnst", [P, KT, 6])
        mv = sb("mv", [P, KT, 2])
        var_eps = sb("var_eps", [P, KT])
        rstd = sb("rstd", [P, KT])
        sumsq = sb("sumsq", [P, KT])
        ms_eps = sb("ms_eps", [P, KT])
        rrms = sb("rrms", [P, KT])
        xhat = sb("xhat", [P, KT, D])
        hmod = sb("hmod", [P, KT, D])
        hmul = sb("hmul", [P, KT, D])
        normed = sb("normed", [P, KT, D])
        mod_bc = sb("mod_bc", [P, 2, 2 * D])
        nT_hi = sb("nT_hi", [P, 2, S], F32R)
        nT_lo = sb("nT_lo", [P, 2, S], F32R)
        qk_hi = sb("qk_hi", [P, 2, 2, S], F32R)
        qk_lo = sb("qk_lo", [P, 2, 2, S], F32R)
        v_sb = sb("v_sb", [P, KT, HD])
        vn = sb("vn", [P, 2, KT, P])
        s_sb = sb("s_sb", [P, 4, SW])
        smin = sb("smin", [P, 4, KT])
        zsum = sb("zsum", [P, 2, KT, 2])
        rz = sb("rz", [P, 2, KT, 2])
        zT_hi = sb("zT_hi", [P, 2, S], F32R)
        zT_lo = sb("zT_lo", [P, 2, S], F32R)
        attT = sb("attT", [P, S])

        memory.close()
        memory = ctx

        act_sb = sb("act_sb", [P, 2, CH])
        prod_sb = sb("prod_sb", [P, 2, CH])
        hid = sb("hid", [P, 3, CH])
        hid_hi = sb("hid_hi", [P, 3, CH], F32R)
        hid_lo = sb("hid_lo", [P, 3, CH], F32R)
        yT = sb("yT", [P, CH])

        banks = [pb(f"bank{i}") for i in range(8)]
        pQK, pS, pZ, pO, pM = banks[0:2], banks[2:4], banks[4], banks[5], banks[6:8]

        x_first = sem("x_first")
        x_loaded = [sem(f"x_loaded{i}") for i in range(3)]
        w_loaded = sem("w_loaded")
        mod_loaded = sem("mod_loaded")
        bias_loaded = sem("bias_loaded")
        consts_made = sem("consts_made")
        pick_made = sem("pick_made")
        padding_made = sem("padding_made")
        silu_c_done = sem("silu_c_done")
        pro_pe = sem("pro_pe")
        pro_ev = sem("pro_ev")
        pro_step = sem("pro_step")
        mod_rows_made = sem("mod_rows_made")
        nbq_made = sem("nbq_made")
        gates_made = sem("gates_made")
        bv_diag_made = sem("bv_diag_made")
        mod_stored = sem("mod_stored")
        bv_rows_made = sem("bv_rows_made")
        w_hi_done = sem("w_hi_done")
        raw_loaded = [sem(f"raw_loaded{i}") for i in range(2)]
        raw_hi = sem("raw_hi")
        raw_lo = sem("raw_lo")
        mod_rows_in = [sem(f"mod_rows_in{i}") for i in range(2)]
        norm_step = sem("norm_step")
        pow_done = sem("pow_done")
        hmod_step = sem("hmod_step")
        normed_done = sem("normed_done")
        nT_ps = sem("nT_ps")
        nT_hi_done = sem("nT_hi_done")
        nT_lo_done = sem("nT_lo_done")
        qk_ps = sem("qk_ps")
        qk_hi_done = sem("qk_hi_done")
        qk_lo_done = sem("qk_lo_done")
        s_ps = sem("s_ps")
        s_masked = sem("s_masked")
        e_done = sem("e_done")
        rz_done = sem("rz_done")
        vn_done = sem("vn_done")
        v_ps = sem("v_ps")
        v_done = sem("v_done")
        z_ps = sem("z_ps")
        z_hi_done = sem("z_hi_done")
        z_lo_done = sem("z_lo_done")
        o_ps = sem("o_ps")
        att_done = sem("att_done")
        attT_ps = sem("attT_ps")
        x_added = sem("x_added")
        ln_step = sem("ln_step")
        pow2_done = sem("pow2_done")
        xT_ps = sem("xT_ps")
        hT_done = sem("hT_done")
        hT_hi_done = sem("hT_hi_done")
        hT_lo_done = sem("hT_lo_done")
        logit_ps = sem("logit_ps")
        sig_done = sem("sig_done")
        route_step = sem("route_step")
        cwT_ps = sem("cwT_ps")
        cwT_done = sem("cwT_done")
        g_ps = sem("g_ps")
        u_ps = sem("u_ps")
        c_ps = sem("c_ps")
        silu_done = sem("silu_done")
        au_done = sem("au_done")
        hid_done = sem("hid_done")
        hid_hi_done = sem("hid_hi_done")
        hid_lo_done = sem("hid_lo_done")
        down_done = sem("down_done")
        yT_done = sem("yT_done")
        yT_ps = sem("yT_ps")
        y_done = sem("y_done")
        y_stored = sem("y_stored")

        rows = stage[:].rearrange("p a n -> p (a n)")
        wq_rows = rows[:, 0:PAIRS * 3 * P].rearrange("p (j c i) -> p j c i", j=PAIRS, c=3)
        wo_rows = rows[:, PAIRS * 3 * P:PAIRS * 4 * P]
        scratch = s_sb[:].rearrange("p a s -> p (a s)")
        wmod_sb = scratch[:, 0:6 * D]
        c_sb = scratch[0:NB, 6 * D:7 * D]
        sc_sb = scratch[0:NB, 7 * D:8 * D]
        gw_rows = scratch[0:E, 8 * D:9 * D]
        scT = scratch[:, 9 * D:9 * D + NB]
        mod_rows = scratch[0:NB, 10 * D:12 * D]
        bv_diag = vn[:].rearrange("p a k n -> p (a k) n")

        def raw_lot(n):
            raw = stage[:, n % 2]
            if n < 2:
                w, a, s = ((w_gate, an_gate, sh_gate), (w_up, an_up, sh_up))[n]
                return [
                    (raw[:, 0:ET * P].rearrange("p (e i) -> p e i", i=EI), w.rearrange("e h i -> h e i")),
                    (raw[:, ET * P:WT * P].rearrange("p (l i) -> p l i", i=AI), a.rearrange("l h i -> h l i")),
                    (raw[:, WT * P:WT * P + EI], s),
                ]
            raw = raw.rearrange("p (t n) -> p t n", n=P)
            return [
                (raw[:, 0:ET, :], w_down.rearrange("(t e) i h -> (e i) t h", e=P // EI)),
                (raw[:, ET:WT, :], an_down.rearrange("(t l) i h -> (l i) t h", l=P // AI)),
                (raw[0:EI, WT, :], sh_down),
            ]

        RAW_LOTS = 3
        PIECE = 3
        PIECES = FT // PIECE
        assert PIECES * PIECE == FT

        def raw_piece(n):
            lot, tiles = n // PIECES, slice(n % PIECES * PIECE, (n % PIECES + 1) * PIECE)
            hi, lo = (wd_hi[:], wd_lo[:]) if lot == 2 else (wgu_hi[:, lot], wgu_lo[:, lot])
            raw = stage[:, lot % 2].rearrange("p (t n) -> p t n", n=P)
            return raw[:, tiles, :], hi[:, tiles, :], lo[:, tiles, :]

        def raw_pieces(g):
            two = RAW_LOTS * PIECES - 2 * PAIRS
            if not isinstance(g, int) or not 0 <= g < 2 * PAIRS:
                return ()
            return (g,) if g < 2 * PAIRS - two else (2 * g - (2 * PAIRS - two), 2 * g - (2 * PAIRS - two) + 1)

        block = ctx.enter_context(nc.Block())
        last_b = NB - 1

        def each_sequence(eng, body):
            body(0, 0)
            body(1, 1)
            with eng.Fori(1, NB // 2 - 1) as i:
                body(i * 2, 0)
                body(i * 2 + 1, 1)
            body(NB - 2, 0)
            body(NB - 1, 1)

        def is_first(b):
            return isinstance(b, int) and b == 0

        def is_last(b):
            return isinstance(b, int) and b == last_b

        def each_chunk(eng, body):
            body(0, 0)
            body(1, 1)
            with eng.Fori(1, NCH // 2 - 1) as i:
                body(i * 2, 0)
                body(i * 2 + 1, 1)
            body(NCH - 2, 0)
            body(NCH - 1, 1)

        def wait_apart(eng, semaphore, count, cell):
            eng.wait_ge(semaphore, count)
            if not isinstance(count, int):
                eng.memset(unused[:, cell:cell + 1], 0.0)

        def below(n, limit):
            return isinstance(n, int) and n < limit


        pG, pU, pC, pY, pX = banks[0:2], banks[2:4], banks[4:6], banks[6], banks[7]
        LN_AT, INPUT_AT, LOGITS_AT = 0, 2, 4
        ROUTE_FIRST = [(0, 3), (3, 5), (5, 6)]
        LN_STEPS = 13
        ROUTE_STEPS = 32

        def three(pe, dst, lhs_hi, lhs_lo, rhs_hi, rhs_lo, start=True, stop=True):
            pe.matmul(dst, lhs_hi, rhs_hi, start=start, stop=False)
            pe.matmul(dst, lhs_hi, rhs_lo, start=False, stop=False)
            return pe.matmul(dst, lhs_lo, rhs_hi, start=False, stop=stop)

        def ln_rstd(pool, c):
            pool.wait_ge(ln_step, c * LN_STEPS + 9)
            pool.tensor_tensor(rstd2[:], var_eps2[:], half_pow[:], ALU.pow).then_inc(pow2_done, 1)

        def input_low(pool, c, par):
            pool.wait_ge(hT_hi_done, c + 1)
            pool.tensor_tensor(hT_lo[:, par], hT, hT_hi[:, par].bitcast(F32), ALU.subtract).then_inc(hT_lo_done, 1)

        def input_transposes(pe, c):
            pe.wait_ge(ln_step, c * LN_STEPS + LN_STEPS)
            for k in range(TPC):
                ins = pe.transpose(pX[:, k * P:(k + 1) * P], xhat2[:, k, :], ident[:])
            ins.then_inc(xT_ps, 1)

        def logits(pe, c, par):
            pe.wait_ge(hT_lo_done, c + 1)
            for k in range(TPC):
                toks = slice(k * P, (k + 1) * P)
                ins = three(pe, pX[:, k * E:(k + 1) * E], hT_hi[:, par, toks], hT_lo[:, par, toks], gwT_hi[:], gwT_lo[:])
            ins.then_inc(logit_ps, 1)

        def weight_transposes(pe, c):
            pe.wait_ge(route_step, c * ROUTE_STEPS + ROUTE_STEPS)
            for k in range(TPC):
                ins = pe.transpose(pX[0:2 * RW, k * P:(k + 1) * P], cw_parts[:, k, :].bitcast(F32), ident[:])
            ins.then_inc(cwT_ps, 1)

        def input_high(act, c, par):
            act.wait_ge(hT_done, c * 2 + 2)
            act.activation(hT_hi[:, par], hT, ACT.Copy).then_inc(hT_hi_done, 1)

        def scores_out(act, c):
            act.wait_ge(logit_ps, c + 1)
            act.activation(sig[:], pX[:, 0:TPC * E].rearrange("p (k e) -> p k e", k=TPC), ACT.Sigmoid).then_inc(sig_done, 1)

        def weights_in(act, c, par):
            act.wait_ge(cwT_ps, c + 1)
            act.activation(cwT[:, par, :], pX[0:2 * RW, :], ACT.Copy).then_inc(cwT_done, 1)

        ROUTE_AT = [0, 3, 7, 12, 16, 18, 20, 21, 22, 27, 32]
        ROUTE_PARTS = len(ROUTE_AT) - 1
        LARGEST = 17

        def layer_norm(dve, c, part):
            def xt(k):
                return x_all[:, bass.ds(c * TPC + k, 1), :].rearrange("p a d -> p (a d)")

            base = c * LN_STEPS
            if part < 2:
                for k in range(part * 2, part * 2 + 2):
                    dve.bn_stats(bnst2[:, k, :], xt(k)).then_inc(ln_step, 1)
            if part == 1:
                wait_apart(dve, ln_step, base + 4, 5)
                for k in range(TPC):
                    dve.bn_aggr(mv2[:, k, :], bnst2[:, k, :]).then_inc(ln_step, 1)
                dve.wait_ge(ln_step, base + 8)
                dve.tensor_scalar(var_eps2[:], mv2[:, :, 1], LN_EPS, None, ALU.add).then_inc(ln_step, 1)
            if part >= 2:
                dve.wait_ge(pow2_done, c + 1)
                for k in range(part * 2 - 4, part * 2 - 2):
                    dve.tensor_scalar(xhat2[:, k, :], xt(k), mv2[:, k, 0:1], rstd2[:, k:k + 1],
                                      ALU.subtract, ALU.mult).then_inc(ln_step, 1)

        def input_out(dve, c):
            dve.wait_ge(xT_ps, c + 1)
            for s in range(SPC):
                toks = slice(s * S, (s + 1) * S)
                dve.tensor_scalar(hT[:, toks], pX[:, toks], modT[:, 4, bass.ds(c * SPC + s, 1)],
                                  modT[:, 3, bass.ds(c * SPC + s, 1)], ALU.mult, ALU.add).then_inc(hT_done, 1)

        def route(dve, c, part):
            base = c * ROUTE_STEPS
            G8 = E // N_GROUP
            grouped = sel[:].rearrange("p k (g e) -> p (k g) e", e=G8)
            m1, m2, cnt, t1, t2, rank = [gtop[:, i].rearrange("p k g -> p (k g)") for i in range(6)]
            four = [P, TPC, N_GROUP, N_GROUP]
            theirs = gtop[:, 0].rearrange("p k (a i) -> p k a i", a=1).broadcast_to(four)
            own = gtop[:, 0].rearrange("p k (j a) -> p k j a", a=1).broadcast_to(four)
            early = earlier[:].rearrange("p (a j) i -> p a j i", a=1).broadcast_to(four)
            bias = bias_row[:].rearrange("p (a e) -> p a e", a=1).broadcast_to([P, TPC, E])
            scale = wsum[:, 1].rearrange("p (k a) -> p k a", a=1).broadcast_to([P, TPC, E])
            experts = iota_e[:].rearrange("p (a e) -> p a e", a=1).broadcast_to([P, TPC * TOP_K, E])
            places_of = idxf[:].rearrange("p k (i a) -> p (k i) a", a=1).broadcast_to([P, TPC * TOP_K, E])

            def over_e(v):
                return v.rearrange("p (a b) -> p a b", b=1).broadcast_to([P, TPC * N_GROUP, G8])

            def largest(k):
                return dve.max(top8[:, k, :], masked[:, k, :])

            def places(k):
                return dve.max_index(idx8[:, k, :], top8[:, k, :], masked[:, k, :])

            def per_tile(f):
                return [f(k) for k in range(TPC)][-1]

            steps = [
                lambda: dve.tensor_tensor(sel[:], sig[:], bias, ALU.add),
                lambda: dve.tensor_reduce(m1, grouped, AX_X, ALU.max),
                lambda: dve.tensor_tensor(dup[:], grouped, over_e(m1), ALU.is_equal),
                lambda: dve.tensor_reduce(cnt, dup[:], AX_X, ALU.add),
                lambda: dve.scalar_tensor_tensor(out=dup[:], in0=dup[:], scalar=-BIG, in1=grouped, op0=ALU.mult, op1=ALU.add),
                lambda: dve.tensor_reduce(m2, dup[:], AX_X, ALU.max),
                lambda: dve.tensor_scalar(t1, cnt, 1.5, BIG, ALU.is_ge, ALU.mult),
                lambda: dve.scalar_tensor_tensor(out=t2, in0=t1, scalar=-BIG, in1=m1, op0=ALU.add, op1=ALU.add),
                lambda: dve.tensor_tensor(m2, m2, t2, ALU.max),
                lambda: dve.tensor_tensor(m1, m1, m2, ALU.add),
                lambda: dve.tensor_tensor(ge4[:], theirs, own, ALU.is_ge),
                lambda: dve.tensor_tensor(gt4[:], theirs, own, ALU.is_gt),
                lambda: dve.tensor_tensor(ge4[:], ge4[:], early, ALU.mult),
                lambda: dve.tensor_tensor(gt4[:], gt4[:], ge4[:], ALU.max),
                lambda: dve.tensor_reduce(rank, gt4[:].rearrange("p k j i -> p (k j) i"), AX_X, ALU.add),
                lambda: dve.tensor_scalar(t1, rank, 1.5, -BIG, ALU.is_ge, ALU.mult),
                lambda: dve.tensor_tensor(masked[:].rearrange("p k (g e) -> p (k g) e", e=G8), grouped, over_e(t1), ALU.add),
                lambda: per_tile(largest),
                lambda: per_tile(places),
                lambda: dve.tensor_copy(idxf[:], idx8[:, :, 0:TOP_K]),
                lambda: dve.tensor_tensor(chosen[:].rearrange("p k i e -> p (k i) e"), experts, places_of, ALU.is_equal),
                lambda: dve.tensor_reduce(masked[:], chosen[:].rearrange("p k i e -> p k e i"), AX_X, ALU.add),
                lambda: dve.tensor_tensor(masked[:], masked[:], sig[:], ALU.mult),
                lambda: dve.tensor_reduce(wsum[:, 0], masked[:], AX_X, ALU.add),
                lambda: dve.tensor_scalar(wsum[:, 1], wsum[:, 0], 1e-20, None, ALU.add),
                lambda: dve.reciprocal(wsum[:, 0], wsum[:, 1]),
                lambda: dve.tensor_scalar(wsum[:, 1], wsum[:, 0], ROUTED_SCALE, None, ALU.mult),
                lambda: dve.tensor_tensor(cw[:, :, 0:E], masked[:], scale, ALU.mult),
                lambda: dve.tensor_tensor(cw[:, :, E:RW], chosen[:, :, 0, 0:E:2], chosen[:, :, 0, 1:E:2], ALU.add),
                lambda: dve.tensor_scalar(cw[:, :, E:RW], cw[:, :, E:RW], ANCHOR_ALPHA, None, ALU.mult),
                lambda: dve.tensor_copy(cw_parts[:, :, 0:RW], cw[:]),
                lambda: dve.tensor_tensor(cw_parts[:, :, RW:2 * RW], cw[:], cw_parts[:, :, 0:RW].bitcast(F32), ALU.subtract),
            ]
            assert len(steps) == ROUTE_STEPS
            if part == 0:
                dve.wait_ge(sig_done, c + 1)
            for n in range(ROUTE_AT[part], ROUTE_AT[part + 1]):
                if n in (LARGEST, LARGEST + 1):
                    wait_apart(dve, route_step, base + n, 6 + n - LARGEST)
                elif n:
                    dve.wait_ge(route_step, base + n)
                steps[n]().then_inc(route_step, 1)

        def ffn_pool(pool):
            pool.wait_ge(x_added, NB)

            def hidden_low(T, t):
                pool.wait_ge(hid_hi_done, T + 1)
                if not below(T, 3):
                    pool.wait_ge(down_done, T - 2)
                pool.tensor_tensor(hid_lo[:, t % 3], hid[:, t % 3], hid_hi[:, t % 3].bitcast(F32),
                                   ALU.subtract).then_inc(hid_lo_done, 1)

            def chunk(c, par):
                for t in range(FT):
                    if not (isinstance(c, int) and c == NCH - 1):
                        if t == 2:
                            ln_rstd(pool, c + 1)
                        if t == 7:
                            input_low(pool, c + 1, 1 - par)
                    hidden_low(c * FT + t, t)

            each_chunk(pool, chunk)

        def ffn_tensor(pe):
            pe.wait_ge(x_added, NB)
            pe.wait_ge(raw_lo, RAW_LOTS * PIECES)

            def gate_up(T, t, par, q):
                for w, (dst, free, done) in enumerate(((pG[q], silu_done, g_ps), (pU[q], au_done, u_ps))):
                    if not below(T, 2):
                        pe.wait_ge(free, T - 1)
                    three(pe, dst[:], wgu_hi[:, w, t, :], wgu_lo[:, w, t, :], hT_hi[:, par], hT_lo[:, par]).then_inc(done, 1)

            def weights_out(T, t, par, c):
                if t >= 2:
                    pe.wait_ge(hid_done, T - 1)
                elif not below(T, FT):
                    pe.wait_ge(hid_done, T - 2)
                if t == 0:
                    pe.wait_ge(cwT_done, c + 1)
                pe.matmul(pC[t % 2][:], pick[0:2 * RW, t, :], cwT[:, par, :], start=True, stop=True).then_inc(c_ps, 1)

            def down(T, t, c):
                pe.wait_ge(hid_lo_done, T + 1)
                if t == 0 and not (isinstance(c, int) and c == 0):
                    pe.wait_ge(yT_done, c)
                K = P if t < WT else EI
                three(pe, pY[:], wd_hi[0:K, t, :], wd_lo[0:K, t, :], hid_hi[0:K, t % 3], hid_lo[0:K, t % 3],
                      start=(t == 0), stop=(t == FT - 1)).then_inc(down_done, 1)

            def result_transposes(c):
                pe.wait_ge(yT_done, c + 1)
                if not (isinstance(c, int) and c == NCH - 1):
                    pe.wait_ge(cwT_done, c + 2)
                for k in range(TPC):
                    ins = pe.transpose(pX[:, k * P:(k + 1) * P], yT[:, k * P:(k + 1) * P], ident[:])
                ins.then_inc(yT_ps, 1)

            def chunk(c, par):
                first, last = isinstance(c, int) and c == 0, isinstance(c, int) and c == NCH - 1
                for t in range(FT):
                    T = c * FT + t
                    gate_up(T, t, par, (FT * par + t) % 2)
                    if t == 0:
                        weight_transposes(pe, c)
                        if not first:
                            down(T - 3, FT - 3, c - 1)
                    if t < WT:
                        weights_out(T, t, par, c)
                    if t >= 3:
                        down(T - 3, t - 3, c)
                    elif t and not first:
                        down(T - 3, t - 3 + FT, c - 1)
                    if t == 4 and not first:
                        result_transposes(c - 1)
                    if not last:
                        if t == 6:
                            if not first:
                                pe.wait_ge(y_done, c)
                            input_transposes(pe, c + 1)
                        if t == 9:
                            logits(pe, c + 1, 1 - par)

            each_chunk(pe, chunk)
            for t in (FT - 3, FT - 2, FT - 1):
                down((NCH - 1) * FT + t, t, NCH - 1)
            pe.wait_ge(y_done, NCH - 1)
            result_transposes(NCH - 1)

        def ffn_scalar(act):
            act.wait_ge(x_added, NB)

            def gate_silu(T, q):
                act.wait_ge(g_ps, T + 1)
                if not below(T, 2):
                    act.wait_ge(au_done, T - 1)
                act.activation(act_sb[:, q], pG[q][:], ACT.Silu).then_inc(silu_done, 1)

            def hidden_high(T, t):
                act.wait_ge(hid_done, T + 1)
                if not below(T, 3):
                    act.wait_ge(down_done, T - 2)
                act.activation(hid_hi[:, t % 3], hid[:, t % 3], ACT.Copy).then_inc(hid_hi_done, 1)

            def result_out(c):
                act.wait_ge(down_done, c * FT + FT)
                for s in range(SPC):
                    toks = slice(s * S, (s + 1) * S)
                    ins = act.activation(yT[:, toks], pY[:, toks], ACT.Copy, scale=gbT[:, bass.ds(c * SPC + s, 1)])
                ins.then_inc(yT_done, 1)

            def chunk(c, par):
                first, last = isinstance(c, int) and c == 0, isinstance(c, int) and c == NCH - 1
                for t in range(FT):
                    T = c * FT + t
                    if t == 3 and not first:
                        result_out(c - 1)
                    gate_silu(T, (FT * par + t) % 2)
                    if t == 0:
                        weights_in(act, c, par)
                    if t:
                        hidden_high(T - 1, t - 1)
                    elif not first:
                        hidden_high(T - 1, FT - 1)
                    if not last:
                        if t == 7:
                            input_high(act, c + 1, 1 - par)
                        if t == 10:
                            scores_out(act, c + 1)

            each_chunk(act, chunk)
            hidden_high(NCH * FT - 1, FT - 1)
            result_out(NCH - 1)

        def ffn_vector(dve):
            def hidden(T, t, q):
                dve.wait_ge(silu_done, T + 1)
                dve.wait_ge(u_ps, T + 1)
                dve.tensor_tensor(prod_sb[:, q], pU[q][:], act_sb[:, q], ALU.mult).then_inc(au_done, 1)

            def weigh(T, t, q, c):
                dve.wait_ge(au_done, T + 1)
                if not below(T, 3):
                    dve.wait_ge(hid_lo_done, T - 2)
                if t == WT:
                    dve.tensor_copy(hid[:, t % 3], prod_sb[:, q]).then_inc(hid_done, 1)
                    return
                dve.wait_ge(c_ps, c * WT + (t + 1))
                dve.tensor_tensor(hid[:, t % 3], pC[t % 2][:], prod_sb[:, q], ALU.mult).then_inc(hid_done, 1)

            def residual_out(c):
                dve.wait_ge(yT_ps, c + 1)
                t = x_all[:, bass.ds(c * TPC, TPC), :]
                dve.tensor_tensor(t, pX[:].rearrange("p (k d) -> p k d", k=TPC), t, ALU.add).then_inc(y_done, 1)

            dve.wait_ge(x_added, NB)
            def chunk(c, par):
                first, last = isinstance(c, int) and c == 0, isinstance(c, int) and c == NCH - 1
                for t in range(FT):
                    q = (FT * par + t) % 2
                    T = c * FT + t
                    hidden(T, t, q)
                    if t == 5 and not first:
                        residual_out(c - 1)
                    if not last:
                        if t in (0, 1, 4, 5):
                            layer_norm(dve, c + 1, (0, 1, 2, 2, 2, 3)[t])
                        if t == 7:
                            input_out(dve, c + 1)
                        if 10 <= t < 10 + ROUTE_PARTS:
                            route(dve, c + 1, t - 10)
                    weigh(T, t, q, c)

            each_chunk(dve, chunk)
            residual_out(NCH - 1)

        W_BANKS = PAIRS

        def attention_weights(n):
            jj = n // 3 * 4 if n < 6 else (n - 6) * 4
            what = n % 3 if n < 6 else 3
            if what < 2:
                parts = wqk_hi[:, what, jj:jj + 4, :], wqk_lo[:, what, jj:jj + 4, :]
            elif what == 2:
                return wv_hi[:, jj * P:(jj + 4) * P], wv_lo[:, jj * P:(jj + 4) * P], 1.0
            else:
                parts = woT_hi[:, jj:jj + 4, :], woT_lo[:, jj:jj + 4, :]
            hi, lo = (w.rearrange("p j n -> p (j n)") for w in parts)
            return hi, lo, -1.0 if what == 0 else 1.0

        def prologue_dve(dve, norm_part):
            steps, seen = [0], [0]

            def then(ins):
                steps[0] += 1
                ins.then_inc(pro_step, 1)
                dve.wait_ge(pro_step, steps[0])

            def bank():
                if seen[0] == 4:
                    seen[0] = 5
                seen[0] += 1
                dve.wait_ge(pro_pe, seen[0])
                return banks[(seen[0] - 1) % 8]

            def bias_diagonals(half):
                if half:
                    dve.wait_ge(pro_pe, 5)
                else:
                    dve.wait_ge(bias_loaded, 48)
                    dve.wait_ge(consts_made, 6)
                four = [P, 4, P]
                dve.tensor_tensor(bv_diag, ident[:].rearrange("p (a n) -> p a n", a=1).broadcast_to(four),
                                  bqkv[:, half * 4:half * 4 + 4, 2:3].broadcast_to(four), ALU.mult).then_inc(bv_diag_made, 1)

            dve.tensor_copy(scT, bank()[:, 0:NB]).then_inc(pro_ev, 1)
            t = bank()
            then(dve.tensor_copy(gwT_hi[:], t[:, 0:E]))
            dve.tensor_tensor(gwT_lo[:], t[:, 0:E], gwT_hi[:].bitcast(F32), ALU.subtract).then_inc(pro_ev, 1)
            t = bank()
            dve.tensor_scalar(mod_rows[:, 0:D], t[0:NB, D:2 * D], 1.0, None, ALU.add).then_inc(mod_rows_made, 1)
            dve.tensor_copy(mod_rows[:, D:2 * D], t[0:NB, 0:D]).then_inc(mod_rows_made, 1)
            dve.wait_ge(mod_rows_made, 2)
            dve.engine_nop().then_inc(pro_ev, 1)
            norm_part(0)
            bias_diagonals(0)
            dve.tensor_scalar(nbq[:], bqkv[:, :, 0], -1.0, None, ALU.mult).then_inc(nbq_made, 1)
            dve.wait_ge(nbq_made, 1)
            t = bank()
            then(dve.tensor_copy(modT[:], t[:, 0:6 * NB].rearrange("p (m b) -> p m b", m=6)))
            dve.engine_nop().then_inc(pro_ev, 1)
            bias_diagonals(1)
            norm_part(1)
            for n in range(W_BANKS):
                hi, lo, sign = attention_weights(n)
                t = bank()
                dve.wait_ge(w_hi_done, n + 1)
                dve.scalar_tensor_tensor(out=lo, in0=t[:], scalar=sign, in1=hi.bitcast(F32), op0=ALU.mult,
                                         op1=ALU.subtract).then_inc(pro_ev, 1)
                if n == 1:
                    norm_part(2)
                if n == 4:
                    norm_part(3)
            return then

        def gates(dve, then):
            then(dve.tensor_scalar(modT[:, 4], modT[:, 4], 1.0, None, ALU.add))
            for m, dst in ((2, gaT), (5, gbT)):
                g = modT[:, m]
                then(dve.scalar_tensor_tensor(out=mod_tmp[:, 0], in0=g, scalar=-1.0, in1=g, op0=ALU.mult, op1=ALU.max))
                then(dve.tensor_scalar(mod_tmp[:, 0], mod_tmp[:, 0], 0.25, None, ALU.max))
                then(dve.tensor_scalar(mod_tmp[:, 1], g, 0.0, 2.0, ALU.is_ge, ALU.mult))
                then(dve.scalar_tensor_tensor(out=dst[:], in0=mod_tmp[:, 1], scalar=-1.0, in1=mod_tmp[:, 0], op0=ALU.add, op1=ALU.mult))
            dve.tensor_scalar(bogaT[:], gaT[:], bo_col[:, 0:1], None, ALU.mult).then_inc(gates_made, 1)

        @block.sync
        def _(sp):
            sp.dma_start(c_sb, cond).then_inc(mod_loaded, 16)
            sp.dma_start(wmod_sb, wmod).then_inc(mod_loaded, 16)
            sp.dma_start(gw_rows, gate_w).then_inc(mod_loaded, 16)
            sp.dma_start(x_all[:, 0:2 * KT, :], x[0:2].rearrange("b (k p) d -> p (b k) d", p=P)).then_inc(x_first, 16)
            sp.dma_start(bqkv[:], b_qkv.rearrange("(j n c) -> n j c", n=P, c=3)).then_inc(bias_loaded, 16)
            sp.dma_start(bo_col[:], b_o.rearrange("(n a) -> n a", a=1)).then_inc(bias_loaded, 16)
            sp.dma_start(bias_row[:], gate_bias.rearrange("(a n) -> a n", a=1).broadcast_to([P, E])).then_inc(bias_loaded, 16)
            sp.dma_start(wq_rows, W_qkv.rearrange("(j n c) i -> n j c i", n=P, c=3)).then_inc(w_loaded, 16)
            sp.dma_start(wo_rows, W_o).then_inc(w_loaded, 16)
            sp.wait_ge(mod_rows_made, 2)
            sp.dma_start(mod_dram, mod_rows).then_inc(mod_stored, 16)
            sp.wait_ge(mod_stored, 16)

            def mod_rows_load(b, par):
                sp.dma_start(mod_bc[:, par, :], mod_dram[bass.ds(b, 1), :].broadcast_to([P, 2 * D])).then_inc(mod_rows_in[par], 16)

            mod_rows_load(0, 0)
            mod_rows_load(1, 1)
            per = (NB - 2) // 3

            def x_load(n):
                b0 = 2 + n * per
                sp.dma_start(x_all[:, b0 * KT:(b0 + per) * KT, :],
                             x[b0:b0 + per].rearrange("b (k p) d -> p (b k) d", p=P)).then_inc(x_loaded[n], 16)

            x_load(0)
            sp.wait_ge(padding_made, 1)
            for n in range(RAW_LOTS):
                if n == 2:
                    x_load(1)
                    x_load(2)
                    sp.wait_ge(raw_lo, PIECES)
                for dst, src in raw_lot(n):
                    sp.dma_start(dst, src).then_inc(raw_loaded[n % 2], 16)

            with sp.Fori(1, NB // 2) as i:
                for k in range(2):
                    sp.wait_ge(hmod_step, i * 4 + (2 * k - 2))
                    mod_rows_load(i * 2 + k, k)

            out_v = out.rearrange("b (k p) d -> p (b k) d", p=P)
            with sp.Fori(0, NCH) as c:
                sp.wait_ge(y_done, c + 1)
                sp.dma_start(out_v[:, bass.ds(c * TPC, TPC), :], x_all[:, bass.ds(c * TPC, TPC), :]).then_inc(y_stored, 16)
            sp.wait_ge(y_stored, 16 * NCH)

        @block.gpsimd
        def _(pool):
            pool.memset(ones[:], 1.0).then_inc(consts_made, 1)
            pool.memset(ident[:], 0.0).then_inc(pick_made, 1)
            pool.memset(causal[:], 0.0).then_inc(pick_made, 1)
            pool.memset(half_pow[:], -0.5).then_inc(consts_made, 1)
            pool.memset(earlier[:], 1.0).then_inc(pick_made, 1)
            pool.wait_ge(pick_made, 3)
            pool.affine_select(out=ident[:], in_=ident[:], compare_op=ALU.not_equal, fill=1.0, base=0,
                               pattern=[[-1, P]], channel_multiplier=1).then_inc(consts_made, 1)
            pool.affine_select(out=causal[:, 0:S], in_=causal[:, 0:S], compare_op=ALU.is_ge, fill=BIG, base=0,
                               pattern=[[1, S]], channel_multiplier=-1)
            pool.affine_select(out=causal[:, S:SW], in_=causal[:, S:SW], compare_op=ALU.is_ge, fill=BIG, base=0,
                               pattern=[[1, P]], channel_multiplier=-1).then_inc(consts_made, 1)
            pool.affine_select(out=earlier[:], in_=earlier[:], compare_op=ALU.is_ge, fill=0.0, base=-1,
                               pattern=[[1, N_GROUP], [-1, N_GROUP]], channel_multiplier=0).then_inc(consts_made, 1)
            pool.iota(iota_e[:], pattern=[[1, E]], base=0, channel_multiplier=0,
                      allow_small_or_imprecise_dtypes=True).then_inc(consts_made, 1)

            def rstd_of(b, par):
                pool.wait_ge(norm_step, b * NORM_STEPS + 5)
                pool.tensor_tensor(rstd[:], var_eps[:], half_pow[:, 0:KT], ALU.pow).then_inc(pow_done, 1)

            def modulate(b, par):
                pool.wait_ge(norm_step, b * NORM_STEPS + 7)
                pool.wait_ge(mod_rows_in[par], b * 8 + (16 - 8 * par))
                m = mod_bc[:, par, :].rearrange("p (a k d) -> p a k d", a=2, k=1)
                pool.tensor_tensor(hmul[:], xhat[:, 0:KT, :], m[:, 0].broadcast_to([P, KT, D]), ALU.mult).then_inc(hmod_step, 1)
                pool.wait_ge(hmod_step, b * 2 + 1)
                pool.tensor_tensor(hmod[:], hmul[:], m[:, 1].broadcast_to([P, KT, D]), ALU.add).then_inc(hmod_step, 1)

            def normalize(b, par):
                pool.wait_ge(norm_step, b * NORM_STEPS + NORM_STEPS)
                pool.tensor_tensor(rrms[:], ms_eps[:], half_pow[:, 0:KT], ALU.pow).then_inc(pow_done, 1)
                pool.wait_ge(pow_done, b * 2 + 2)
                if not is_first(b):
                    pool.wait_ge(nT_ps, b)
                pool.tensor_tensor(normed[:], hmod[:], rrms[:].rearrange("p (k a) -> p k a", a=1).broadcast_to([P, KT, D]),
                                   ALU.mult).then_inc(normed_done, 1)

            def scale_v(g, j, par, v_need):
                pool.wait_ge(rz_done, g + 1)
                pool.wait_ge(v_done, v_need)
                if not (isinstance(g, int) and g < 2):
                    pool.wait_ge(z_ps, g - 1)
                pool.tensor_tensor(
                    vn[:, j % 2].rearrange("p k (h d) -> p k h d", d=DH),
                    v_sb[:, :, j * P:(j + 1) * P].rearrange("p k (h d) -> p k h d", d=DH),
                    rz[:, j % 2].rearrange("p k (h a) -> p k h a", a=1).broadcast_to([P, KT, 2, DH]),
                    ALU.mult).then_inc(vn_done, 1)

            rstd_of(0, 0)
            modulate(0, 0)
            normalize(0, 0)
            pool.wait_ge(pro_pe, 5 + W_BANKS)
            pool.memset(stage[:, :, WT * P:FT * P], 0.0).then_inc(padding_made, 1)
            pool.memset(pick[:].bitcast(F32), 0.0).then_inc(pick_made, 1)
            pool.wait_ge(pick_made, 4)
            for n, (t0, nt, first, per) in enumerate(((0, ET, 0, P // EI), (ET, AT, E, P // AI))):
                v = pick[:, t0:t0 + nt, :].rearrange("p t (w n) -> p t w n", w=per)
                for part in range(2):
                    pool.affine_select(out=v, in_=v, compare_op=ALU.not_equal, fill=1.0, base=-first - part * RW,
                                       pattern=[[-per, nt], [-1, per], [0, P // per]],
                                       channel_multiplier=1).then_inc(pick_made, 1)
                    pool.wait_ge(pick_made, 5 + 2 * n + part)

            def split_low(n):
                raw, hi, lo = raw_piece(n)
                pool.wait_ge(raw_hi, n + 1)
                pool.tensor_tensor(lo, raw, hi.bitcast(F32), ALU.subtract).then_inc(raw_lo, 1)

            def sequence(b, par):
                for j in range(PAIRS):
                    if j:
                        scale_v(b * PAIRS + (j - 1), j - 1, par, b * 4 + (2 if j <= PAIRS // 2 else 4))
                    elif not is_first(b):
                        scale_v(b * PAIRS - 1, PAIRS - 1, 1 - par, b * 4)
                    if not is_last(b):
                        if j == 0:
                            rstd_of(b + 1, 1 - par)
                        if j == 1:
                            modulate(b + 1, 1 - par)
                        if j == 2:
                            normalize(b + 1, 1 - par)
                    elif j == LN_AT:
                        ln_rstd(pool, 0)
                    elif j == INPUT_AT + 1:
                        input_low(pool, 0, 0)
                    for n in raw_pieces(b * PAIRS + (j - 1)):
                        split_low(n)
                    if isinstance(b, int) and b == 1 and j == PAIRS - 1:
                        for n in raw_pieces(2 * PAIRS - 1):
                            split_low(n)

            each_sequence(pool, sequence)
            scale_v(NB * PAIRS - 1, PAIRS - 1, 1, NB * 4)

            ffn_pool(pool)

        def prologue_pe(pe):
            n = [0]

            def bank():
                if n[0] == 12:
                    pe.wait_ge(bv_rows_made, 1)
                elif n[0] >= 8:
                    pe.wait_ge(pro_ev, min(n[0] - 7, 5))
                n[0] += 1
                return banks[(n[0] - 1) % 8]

            pe.wait_ge(consts_made, 6)
            pe.wait_ge(silu_c_done, 1)
            pe.transpose(bank()[:, 0:NB], sc_sb, ident[0:NB, 0:NB]).then_inc(pro_pe, 1)
            pe.wait_ge(mod_loaded, 48)
            pe.transpose(bank()[:, 0:E], gw_rows, ident[0:E, 0:E]).then_inc(pro_pe, 1)
            pe.wait_ge(pro_ev, 1)
            t = bank()
            pe.matmul(t[0:NB, 0:2 * D], scT, wmod_sb[:, 0:2 * D], start=True, stop=True).then_inc(pro_pe, 1)
            t = bank()
            for m in range(6):
                ins = pe.matmul(t[:, m * NB:(m + 1) * NB], wmod_sb[:, m * D:(m + 1) * D], scT, start=True, stop=True)
            ins.then_inc(pro_pe, 1)
            def value_biases(half):
                pe.wait_ge(bv_diag_made, half + 1)
                pe.matmul(bank()[:], ones[:], bv_diag.rearrange("p j n -> p (j n)"), start=True, stop=True).then_inc(pro_pe, 1)

            value_biases(0)
            pe.wait_ge(w_loaded, 32)
            for jj in range(0, PAIRS, 4):
                for c in range(3):
                    t = bank()
                    for k in range(4):
                        ins = pe.transpose(t[:, k * P:(k + 1) * P], wq_rows[:, jj + k, c, :], ident[:])
                    ins.then_inc(pro_pe, 1)
            for jj in range(0, PAIRS, 4):
                t = bank()
                for k in range(4):
                    ins = pe.transpose(t[:, k * P:(k + 1) * P], wo_rows[:, (jj + k) * P:(jj + k + 1) * P], ident[:])
                ins.then_inc(pro_pe, 1)
            value_biases(1)
            pe.wait_ge(pro_ev, 4 + W_BANKS)

        def transpose_normed(pe, b):
            pe.wait_ge(normed_done, b + 1)
            for k in range(KT):
                ins = pe.transpose(pM[1][:, k * P:(k + 1) * P], normed[:, k, :], ident[:])
            ins.then_inc(nT_ps, 1)

        def values(pe, b, par, chunk):
            half, k = chunk // 2, chunk % 2
            if chunk == 0:
                pe.wait_ge(nT_hi_done, b + 1)
                pe.wait_ge(nT_lo_done, b + 1)
                if not (isinstance(b, int) and b < 2):
                    pe.wait_ge(x_added, b - 1)
                elif b == 1:
                    pe.wait_ge(v_done, 3)
            if chunk >= 2:
                pe.wait_ge(v_done, b * 4 + (chunk - 1))
            toks = slice(k * P, (k + 1) * P)
            cols = slice(half * 512, (half + 1) * 512)
            three(pe, pM[chunk % 2][:], nT_hi[:, par, toks], nT_lo[:, par, toks], wv_hi[:, cols], wv_lo[:, cols]).then_inc(v_ps, 1)

        def project(pe, g, j, par):
            if not (isinstance(g, int) and g < 2):
                pe.wait_ge(qk_lo_done, g - 1)
            for w in range(2):
                ins = three(pe, pQK[j % 2][:, w * S:(w + 1) * S], wqk_hi[:, w, j, :], wqk_lo[:, w, j, :],
                            nT_hi[:, par], nT_lo[:, par])
            ins.then_inc(qk_ps, 1)

        def scores(pe, g, j):
            pe.wait_ge(qk_lo_done, g + 1)
            for h in range(2):
                if not (isinstance(g, int) and g == 0):
                    pe.wait_ge(s_masked, g * 2 + (h - 1))
                r = slice(h * DH, (h + 1) * DH)
                t = pS[h]
                for k in range(KT):
                    keys = slice(k * P, (k + 1) * P)
                    dst = t[:, 0:S] if k == 0 else t[:, S:SW]
                    ins = three(pe, dst, qk_hi[r, j % 2, 1, keys], qk_lo[r, j % 2, 1, keys],
                                qk_hi[r, j % 2, 0, k * P:S], qk_lo[r, j % 2, 0, k * P:S])
                ins.then_inc(s_ps, 1)

        def attend(pe, g, j):
            pe.wait_ge(e_done, g * 2 + 2)
            pe.wait_ge(vn_done, g + 1)
            if not (isinstance(g, int) and g == 0):
                pe.wait_ge(z_lo_done, g)
            for k in range(KT):
                for h in range(2):
                    src = s_sb[:, (2 * j + h) % 4, :]
                    ins = pe.matmul(pZ[h * DH:(h + 1) * DH, k * P:S], vn[:, j % 2, k, h * DH:(h + 1) * DH],
                                    src[:, 0:S] if k == 0 else src[:, S:SW], start=(k == 0), stop=(k == KT - 1))
            ins.then_inc(z_ps, 1)

        def project_out(pe, g, j, b):
            pe.wait_ge(z_lo_done, g + 1)
            if j == 0 and not is_first(b):
                pe.wait_ge(att_done, b)
            three(pe, pO[:, 0:S], woT_hi[:, j, :], woT_lo[:, j, :], zT_hi[:, j % 2], zT_lo[:, j % 2],
                  start=(j == 0), stop=(j == PAIRS - 1)).then_inc(o_ps, 1)

        def transpose_att(pe, b):
            pe.wait_ge(att_done, b + 1)
            if is_last(b):
                pe.wait_ge(v_done, NB * 4)
            else:
                pe.wait_ge(v_done, b * 4 + 7)
            for k in range(KT):
                ins = pe.transpose(pM[0][:, k * P:(k + 1) * P], attT[:, k * P:(k + 1) * P], ident[:])
            ins.then_inc(attT_ps, 1)

        @block.tensor
        def _(pe):
            prologue_pe(pe)
            transpose_normed(pe, 0)
            values(pe, 0, 0, 0)
            values(pe, 0, 0, 1)
            project(pe, 0, 0, 0)
            project(pe, 1, 1, 0)

            def sequence(b, par):
                for j in range(PAIRS):
                    g = b * PAIRS + j
                    scores(pe, g, j)
                    if j < 2:
                        values(pe, b, par, 2 + j)
                    if j == 3 and not is_first(b):
                        transpose_att(pe, b - 1)
                    if j == 4 and not is_last(b):
                        pe.wait_ge(v_done, b * 4 + 4)
                        transpose_normed(pe, b + 1)
                    if is_last(b) and j == INPUT_AT:
                        pe.wait_ge(v_done, NB * 4)
                        input_transposes(pe, 0)
                    if is_last(b) and j == LOGITS_AT:
                        logits(pe, 0, 0)
                    if j in (5, 6) and not is_last(b):
                        values(pe, b + 1, 1 - par, j - 5)
                    if j < PAIRS - 2:
                        project(pe, g + 2, j + 2, par)
                    elif not is_last(b):
                        project(pe, g + 2, j + 2 - PAIRS, 1 - par)
                    if j:
                        attend(pe, g - 1, j - 1)
                    elif not is_first(b):
                        attend(pe, g - 1, PAIRS - 1)
                    if j >= 2:
                        project_out(pe, g - 2, j - 2, b)
                    elif not is_first(b):
                        project_out(pe, g - 2, j - 2 + PAIRS, b - 1)

            each_sequence(pe, sequence)
            attend(pe, NB * PAIRS - 1, PAIRS - 1)
            project_out(pe, NB * PAIRS - 2, PAIRS - 2, last_b)
            project_out(pe, NB * PAIRS - 1, PAIRS - 1, last_b)
            transpose_att(pe, last_b)
            ffn_tensor(pe)

        @block.scalar
        def _(act):
            act.wait_ge(mod_loaded, 48)
            act.activation(sc_sb, c_sb, ACT.Silu).then_inc(silu_c_done, 1)
            def value_biases_out(half, n):
                act.wait_ge(pro_pe, n + 1)
                act.activation(bv_rows[:, half * 512:half * 512 + 512], banks[n % 8][:], ACT.Copy).then_inc(bv_rows_made, 1)

            value_biases_out(0, 4)
            for n in range(W_BANKS):
                hi, lo, sign = attention_weights(n)
                act.wait_ge(pro_pe, 6 + n)
                act.activation(hi, banks[(5 + n) % 8][:], ACT.Copy, scale=sign).then_inc(w_hi_done, 1)
            value_biases_out(1, 5 + W_BANKS)

            def normed_hi(b, par):
                act.wait_ge(nT_ps, b + 1)
                act.activation(nT_hi[:, par], pM[1][:, 0:S], ACT.Copy).then_inc(nT_hi_done, 1)

            def qk_high(g, j):
                act.wait_ge(qk_ps, g + 1)
                if not (isinstance(g, int) and g < 2):
                    act.wait_ge(s_ps, g * 2 - 2)
                act.activation(qk_hi[:, j % 2, 0], pQK[j % 2][:, 0:S], ACT.Identity, bias=nbq[:, j:j + 1])
                act.activation(qk_hi[:, j % 2, 1], pQK[j % 2][:, S:2 * S], ACT.Identity,
                               bias=bqkv[:, j, 1:2]).then_inc(qk_hi_done, 1)

            def exponentials(g, j):
                if not (isinstance(g, int) and g < 2):
                    act.wait_ge(rz_done, g - 1)
                for h in range(2):
                    act.wait_ge(s_masked, g * 2 + (h + 1))
                    n = (2 * j + h) % 4
                    for k in range(KT):
                        cols = slice(0, S) if k == 0 else slice(S, SW)
                        ins = act.activation(s_sb[:, n, cols], s_sb[:, n, cols], ACT.Exp, bias=smin[:, n, k:k + 1],
                                             scale=-1.0, accum_out=zsum[:, j % 2, k, h:h + 1])
                    ins.then_inc(e_done, 1)

            def att_out(b):
                act.wait_ge(o_ps, b * PAIRS + PAIRS)
                act.activation(attT[:], pO[:, 0:S], ACT.Identity, scale=gaT[:, bass.ds(b, 1)],
                               bias=bogaT[:, bass.ds(b, 1)]).then_inc(att_done, 1)

            def z_high(g, j):
                act.wait_ge(z_ps, g + 1)
                if not (isinstance(g, int) and g < 2):
                    act.wait_ge(o_ps, g - 1)
                act.activation(zT_hi[:, j % 2], pZ[:, 0:S], ACT.Copy).then_inc(z_hi_done, 1)

            def split_high(n):
                raw, hi, _ = raw_piece(n)
                act.wait_ge(raw_loaded[n // PIECES % 2], 48 * (n // PIECES // 2 + 1))
                act.activation(hi, raw, ACT.Copy).then_inc(raw_hi, 1)

            normed_hi(0, 0)
            act.wait_ge(nbq_made, 1)
            act.wait_ge(bias_loaded, 48)
            qk_high(0, 0)
            qk_high(1, 1)

            def sequence(b, par):
                for j in range(PAIRS):
                    g = b * PAIRS + j
                    if j == 2 and not is_first(b):
                        if isinstance(b, int) and b == 1:
                            act.wait_ge(gates_made, 1)
                        att_out(b - 1)
                    exponentials(g, j)
                    if j or not is_first(b):
                        z_high(g - 1, (j - 1) % PAIRS)
                    if j == 4 and not is_last(b):
                        normed_hi(b + 1, 1 - par)
                    if is_last(b) and j == INPUT_AT:
                        input_high(act, 0, 0)
                    if is_last(b) and j == LOGITS_AT:
                        scores_out(act, 0)
                    if j < PAIRS - 2 or not is_last(b):
                        qk_high(g + 2, (j + 2) % PAIRS)
                    for n in raw_pieces(g):
                        split_high(n)

            each_sequence(act, sequence)
            z_high(NB * PAIRS - 1, PAIRS - 1)
            att_out(last_b)
            ffn_scalar(act)

        @block.vector
        def _(dve):
            def norm(b, par, stage_no):
                base = b * NORM_STEPS
                tiles = [b * KT + k for k in range(KT)]

                def xt(k):
                    return x_all[:, bass.ds(tiles[k], 1), :].rearrange("p a d -> p (a d)")

                if stage_no == 0:
                    for k in range(KT):
                        dve.bn_stats(bnst[:, k, :], xt(k)).then_inc(norm_step, 1)
                    wait_apart(dve, norm_step, base + 2, 4)
                    for k in range(KT):
                        dve.bn_aggr(mv[:, k, :], bnst[:, k, :]).then_inc(norm_step, 1)
                    dve.wait_ge(norm_step, base + 4)
                    dve.tensor_scalar(var_eps[:], mv[:, :, 1], LN_EPS, None, ALU.add).then_inc(norm_step, 1)
                if stage_no == 1:
                    dve.wait_ge(pow_done, b * 2 + 1)
                    for k in range(KT):
                        dve.tensor_scalar(xhat[:, k, :], xt(k), mv[:, k, 0:1], rstd[:, k:k + 1],
                                          ALU.subtract, ALU.mult).then_inc(norm_step, 1)
                if stage_no == 2:
                    dve.wait_ge(hmod_step, b * 2 + 2)
                    for k in range(KT):
                        dve.tensor_tensor_reduce(hmul[:, k, :], hmod[:, k, :], hmod[:, k, :], 1.0, 0.0, ALU.mult,
                                                 ALU.add, sumsq[:, k:k + 1]).then_inc(norm_step, 1)
                    dve.wait_ge(norm_step, base + 9)
                    dve.tensor_scalar(ms_eps[:], sumsq[:], 1.0 / D, RMS_EPS, ALU.mult, ALU.add).then_inc(norm_step, 1)

            def normed_lo(b, par):
                dve.wait_ge(nT_hi_done, b + 1)
                dve.tensor_tensor(nT_lo[:, par], pM[1][:, 0:S], nT_hi[:, par].bitcast(F32), ALU.subtract).then_inc(nT_lo_done, 1)

            def value_rows(b, par, chunk):
                half, k = chunk // 2, chunk % 2
                dve.wait_ge(v_ps, b * 4 + (chunk + 1))
                if not is_first(b):
                    dve.wait_ge(vn_done, b * PAIRS if half else b * PAIRS - PAIRS // 2)
                cols = slice(half * 512, (half + 1) * 512)
                dve.tensor_tensor(v_sb[:, k, cols], pM[chunk % 2][:], bv_rows[:, cols], ALU.add).then_inc(v_done, 1)

            def qk_low(g, j):
                dve.wait_ge(qk_hi_done, g + 1)
                bias = (nbq[:, j:j + 1], bqkv[:, j, 1:2])
                for w in range(2):
                    ins = dve.scalar_tensor_tensor(out=qk_lo[:, j % 2, w], in0=pQK[j % 2][:, w * S:(w + 1) * S],
                                                   scalar=bias[w], in1=qk_hi[:, j % 2, w].bitcast(F32),
                                                   op0=ALU.add, op1=ALU.subtract)
                ins.then_inc(qk_lo_done, 1)

            def z_low(g, j):
                dve.wait_ge(z_hi_done, g + 1)
                dve.tensor_tensor(zT_lo[:, j % 2], pZ[:, 0:S], zT_hi[:, j % 2].bitcast(F32),
                                  ALU.subtract).then_inc(z_lo_done, 1)

            def sums(g, j):
                dve.wait_ge(e_done, g * 2 + 2)
                dve.reciprocal(rz[:, j % 2], zsum[:, j % 2]).then_inc(rz_done, 1)

            def mask_and_min(g, j, heads):
                for h in heads:
                    n = (2 * j + h) % 4
                    if not (isinstance(g, int) and g < 2):
                        dve.wait_ge(z_ps, g - 1)
                    wait_apart(dve, s_ps, g * 2 + (h + 1), n)
                    for k in range(KT):
                        cols = slice(0, S) if k == 0 else slice(S, SW)
                        ins = dve.tensor_tensor_reduce(s_sb[:, n, cols], pS[h][:, cols], causal[:, cols], 1.0, 3e38,
                                                       ALU.add, ALU.min, smin[:, n, k:k + 1])
                    ins.then_inc(s_masked, 1)

            def residual(b):
                dve.wait_ge(attT_ps, b + 1)
                t = x_all[:, bass.ds(b * KT, KT), :]
                dve.tensor_tensor(t, pM[0][:, 0:S].rearrange("p (k d) -> p k d", k=KT), t, ALU.add).then_inc(x_added, 1)

            def first_norm(part):
                if part == 0:
                    dve.wait_ge(x_first, 16)
                norm(part // 3, part // 3, part % 3)

            then = prologue_dve(dve, first_norm)
            dve.wait_ge(bv_rows_made, 2)
            normed_lo(0, 0)
            value_rows(0, 0, 0)
            value_rows(0, 0, 1)
            qk_low(0, 0)

            def sequence(b, par):
                for j in range(PAIRS):
                    g = b * PAIRS + j
                    if j:
                        sums(g - 1, j - 1)
                    elif not is_first(b):
                        sums(g - 1, PAIRS - 1)
                    mask_and_min(g, j, (0,))
                    if j >= 2 or not is_first(b):
                        z_low(g - 2, j)
                    mask_and_min(g, j, (1,))
                    if not (is_last(b) and j == PAIRS - 1):
                        qk_low(g + 1, (j + 1) % PAIRS)
                    if j < 2:
                        value_rows(b, par, 2 + j)
                    if j == 3 and not is_first(b):
                        residual(b - 1)
                    if j == 4 and not is_last(b):
                        normed_lo(b + 1, 1 - par)
                    if j in (5, 6) and not is_last(b):
                        value_rows(b + 1, 1 - par, j - 5)
                    if j < 2 and not is_last(b):
                        norm(b + 1, 1 - par, j + 1)
                    if is_first(b) and j == PAIRS - 1:
                        dve.wait_ge(x_loaded[0], 16)
                    if isinstance(b, int) and b == 1 and j == PAIRS - 1:
                        dve.wait_ge(x_loaded[1], 16)
                        dve.wait_ge(x_loaded[2], 16)
                    if j == PAIRS - 1 and not (isinstance(b, int) and b >= NB - 2):
                        norm(b + 2, par, 0)
                    if is_first(b) and j == 4:
                        gates(dve, then)
                    if is_last(b):
                        if j == 0:
                            dve.wait_ge(raw_lo, RAW_LOTS * PIECES)
                            dve.wait_ge(x_added, SPC)
                            layer_norm(dve, 0, 0)
                            layer_norm(dve, 0, 1)
                        if j == LN_AT + 1:
                            layer_norm(dve, 0, 2)
                            layer_norm(dve, 0, 3)
                        if j == INPUT_AT:
                            input_out(dve, 0)
                        if j > LOGITS_AT:
                            for part in range(*ROUTE_FIRST[j - LOGITS_AT - 1]):
                                route(dve, 0, part)

            each_sequence(dve, sequence)
            sums(NB * PAIRS - 1, PAIRS - 1)
            z_low(NB * PAIRS - 2, PAIRS - 2)
            route(dve, 0, 6)
            route(dve, 0, 7)
            z_low(NB * PAIRS - 1, PAIRS - 1)
            route(dve, 0, 8)
            route(dve, 0, 9)
            residual(last_b)
            ffn_vector(dve)



_INS = ['L0_attn_x', 'L0_attn_W_qkv', 'L0_attn_b_qkv', 'L0_attn_W_o', 'L0_attn_b_o', 'L0_ffn_gate_weight',
        'L0_ffn_gate_bias', 'L0_ffn_w_gate', 'L0_ffn_w_up', 'L0_ffn_w_down', 'L0_ffn_shared_w_gate',
        'L0_ffn_shared_w_up', 'L0_ffn_shared_w_down', 'L0_ffn_anchor_w_gate', 'L0_ffn_anchor_w_up',
        'L0_ffn_anchor_w_down', 'L0_c', 'L0_wmod']


def kernel(**inputs):
    import numpy as _np
    import concourse.bacc as _bacc
    from concourse import mybir as _mybir
    from concourse.bass_utils import run_bass_kernel_spmd as _run

    nc = _bacc.Bacc("TRN2", target_bir_lowering=False, num_devices=1)
    arrays, args = {}, []
    for name in _INS:
        a = _np.ascontiguousarray(inputs[name])
        arrays[f"in_{name}_dram"] = a
        args.append(nc.dram_tensor(f"in_{name}_dram", a.shape, _mybir.dt.from_np(a.dtype), kind="ExternalInput").ap())
    shape = inputs['L0_attn_x'].shape
    args.append(nc.dram_tensor("out_0_dram", shape, _mybir.dt.float32, kind="ExternalOutput").ap())
    adaln_block_kernel(nc, *args)
    r = _run(nc, [arrays], core_ids=[0])
    return r.results[0]["out_0_dram"]
```
